# Optimizing a Trainium2 kernel written in Bass

```python
import numpy as np
import jax
import jax.numpy as jnp

def _softmax(x, axis=-1):
    return jax.nn.softmax(x, axis=axis)

def _gelu(x):
    return jax.nn.gelu(x, approximate=True)

def _silu(x):
    return jax.nn.silu(x)

def _sigmoid(x):
    return jax.nn.sigmoid(x)

def _layernorm(x, axis=-1, eps=1e-05):
    m = jnp.mean(x, axis=axis, keepdims=True)
    v = jnp.var(x, axis=axis, keepdims=True)
    return (x - m) / jnp.sqrt(v + eps)

def _scatter_add(tgt, idx, src, axis=0):
    return tgt.at[idx].add(src)

def _segment_sum(src, seg, n):
    return jax.ops.segment_sum(src, seg, n)
kernel_name = 'mk_gnn_resnorm_d2_gnn_r64_44184e'

def setup_inputs(seed: int=0):
    np.random.seed(seed)
    _w = jnp.asarray

    def _rec_inputs():
        import jax
        import jax.numpy as jnp
        _gk = jax.random.key(seed)
        x = -0.000202 + 1 * jax.random.normal(jax.random.fold_in(_gk, 1), (100000, 128), jnp.float32)
        src = jax.random.randint(jax.random.fold_in(_gk, 2), (25000,), 0, 100000, jnp.int32)
        dst = jnp.minimum((100000 * jax.random.uniform(jax.random.fold_in(_gk, 3), (25000,)) ** 2.0).astype(jnp.int32), 99999)
        _o = jnp.argsort(dst, stable=True)
        src = src[_o]
        dst = dst[_o]
        return (x, src, dst)
    x, src, dst = _rec_inputs()

    def _L0_gnn_setup():
        import jax, jax.numpy as jnp
        import numpy as np
        N_NODES = 50000
        N_EDGES = 9375
        D_IN = 128
        D_OUT = 128
        key = jax.random.key(seed)
        k1, k2, k3, k4 = jax.random.split(key, 4)
        x = jax.random.normal(k1, (N_NODES, D_IN), dtype=jnp.float32)
        edge_index = jax.random.randint(k2, (2, N_EDGES), 0, N_NODES, dtype=jnp.int64)
        W1 = jax.random.normal(k3, (2 * D_IN, D_OUT), dtype=jnp.float32) * (1.0 / np.sqrt(2 * D_IN))
        b1 = jnp.zeros((D_OUT,), dtype=jnp.float32)
        W2 = jax.random.normal(k4, (D_OUT, D_OUT), dtype=jnp.float32) * (1.0 / np.sqrt(D_OUT))
        b2 = jnp.zeros((D_OUT,), dtype=jnp.float32)
        return {'x': x, 'edge_index': edge_index, 'W1': W1, 'b1': b1, 'W2': W2, 'b2': b2}
    _L0_gnn_all = _L0_gnn_setup()
    _L0_gnn_in = {k: v for k, v in _L0_gnn_all.items() if k in ('W1', 'b1', 'W2', 'b2')}
    del _L0_gnn_all

    def _L1_gnn_setup():
        import jax, jax.numpy as jnp
        import numpy as np
        N_NODES = 50000
        N_EDGES = 12500
        D_IN = 128
        D_OUT = 128
        key = jax.random.key(seed)
        ks = jax.random.split(key, 8)
        x = jax.random.normal(ks[0], (N_NODES, D_IN), dtype=jnp.float32)
        edge_index = jax.random.randint(ks[1], (2, N_EDGES), 0, N_NODES, dtype=jnp.int64)
        s = 1.0 / np.sqrt(D_IN)
        so = 1.0 / np.sqrt(D_OUT)
        W1 = jax.random.uniform(ks[2], (D_IN, D_OUT), jnp.float32, -s, s)
        b1 = jax.random.uniform(ks[3], (D_OUT,), jnp.float32, -s, s)
        W2 = jax.random.uniform(ks[4], (D_OUT, D_OUT), jnp.float32, -so, so)
        b2 = jax.random.uniform(ks[5], (D_OUT,), jnp.float32, -so, so)
        Wres = jax.random.uniform(ks[6], (D_IN, D_OUT), jnp.float32, -s, s)
        bres = jax.random.uniform(ks[7], (D_OUT,), jnp.float32, -s, s)
        return {'x': x, 'edge_index': edge_index, 'W1': W1, 'b1': b1, 'W2': W2, 'b2': b2, 'Wres': Wres, 'bres': bres}
    _L1_gnn_all = _L1_gnn_setup()
    _L1_gnn_in = {k: v for k, v in _L1_gnn_all.items() if k in ('W1', 'b1', 'W2', 'b2', 'Wres', 'bres')}
    del _L1_gnn_all
    return {'x': x, 'src': src, 'dst': dst, 'L0_gnn_W1': _L0_gnn_in['W1'], 'L0_gnn_b1': _L0_gnn_in['b1'], 'L0_gnn_W2': _L0_gnn_in['W2'], 'L0_gnn_b2': _L0_gnn_in['b2'], 'L1_gnn_W1': _L1_gnn_in['W1'], 'L1_gnn_b1': _L1_gnn_in['b1'], 'L1_gnn_W2': _L1_gnn_in['W2'], 'L1_gnn_b2': _L1_gnn_in['b2'], 'L1_gnn_Wres': _L1_gnn_in['Wres'], 'L1_gnn_bres': _L1_gnn_in['bres']}

def reference(x, src, dst, L0_gnn_W1, L0_gnn_b1, L0_gnn_W2, L0_gnn_b2, L1_gnn_W1, L1_gnn_b1, L1_gnn_W2, L1_gnn_b2, L1_gnn_Wres, L1_gnn_bres):
    import jax
    import jax.numpy as jnp

    def _L0_gnn_ref(x, edge_index, W1, b1, W2, b2):
        import jax, jax.numpy as jnp
        import numpy as np
        N_NODES = 50000
        N_EDGES = 9375
        D_IN = 128
        D_OUT = 128
        row, col = (edge_index[0], edge_index[1])
        x_col = x[col]
        feat = jnp.concatenate([x_col, x[row] - x_col], axis=-1)
        h = jax.nn.relu(feat @ W1 + b1)
        messages = h @ W2 + b2
        out = jax.ops.segment_max(messages, col, num_segments=x.shape[0])
        out = jnp.where(jnp.isneginf(out), jnp.zeros_like(out), out)
        return out

    def _L1_gnn_ref(x, edge_index, W1, b1, W2, b2, Wres, bres):
        import jax, jax.numpy as jnp
        import numpy as np
        N_NODES = 50000
        N_EDGES = 12500
        D_IN = 128
        D_OUT = 128
        src = edge_index[0]
        dst = edge_index[1]
        agg = jax.ops.segment_sum(x[src], dst, num_segments=x.shape[0])
        h = x + agg
        h = jnp.maximum(h @ W1 + b1, 0.0) @ W2 + b2
        res = x @ Wres + bres
        return res + h
    edge_index = jnp.stack([src, dst])
    x = _layernorm(x + _L0_gnn_ref(x, edge_index, L0_gnn_W1, L0_gnn_b1, L0_gnn_W2, L0_gnn_b2), axis=-1)
    x = _layernorm(x + _L1_gnn_ref(x, edge_index, L1_gnn_W1, L1_gnn_b1, L1_gnn_W2, L1_gnn_b2, L1_gnn_Wres, L1_gnn_bres), axis=-1)
    return x

_drawn_inputs = setup_inputs


def setup_inputs(seed=0):
    import zlib

    import numpy as np

    out = dict(_drawn_inputs(seed))
    spreads = {'L0_gnn_b1': (0.0, 0.32), 'L0_gnn_b2': (0.0, 0.1)}
    factors = {'L1_gnn_b1': 3.307}
    for name, (base, spread) in spreads.items():
        noise = np.random.default_rng([zlib.crc32(name.encode()), seed]).standard_normal(out[name].shape)
        drawn = base * np.exp(spread * noise) if base else spread * noise
        out[name] = jnp.asarray(drawn.astype(out[name].dtype))
    for name, factor in factors.items():
        out[name] = (out[name] * factor).astype(out[name].dtype)
    return out
```

```python
from contextlib import ExitStack

import concourse.bass as bass
from concourse import mybir

FP32 = mybir.dt.float32
BF16 = mybir.dt.bfloat16
I32 = mybir.dt.int32
ALU = mybir.AluOpType
ACT = mybir.ActivationFunctionType
AX = mybir.AxisListType

P = 128
EPS = 1e-5
TILES = 4
ROWS = TILES * P
SLOTS = 4
BIG = 1 << 21
LOWEST = -3.0e38
ZERO_CHUNK = 1250


def gnn_program(nc, x, src, dst, e_w1, e_b1, e_w2, e_b2, w1, b1, w2, b2, wres, bres, out):
    N, D = x.shape
    E = src.shape[0]
    UNITS = -(-N // ROWS)
    BODIES = UNITS // SLOTS
    assert UNITS == BODIES * SLOTS and N % 32 == 0
    GROUPS = 2 * -(-E // (2 * ROWS))
    PAIRS = GROUPS // 2
    ETILES = GROUPS * TILES
    FULL = E // P
    REST = E - FULL * P
    FIRST_A = 16
    FIRST_B = FIRST_A + PAIRS
    LAST = BODIES - 1
    PAIRS_B1 = BODIES - FIRST_B
    ZCH = N * D // P // ZERO_CHUNK

    ctx = ExitStack()
    with ctx:
        def sb(name, shape, dt=FP32):
            return ctx.enter_context(nc.sbuf_tensor(name, shape, dt))

        def ps(name):
            return ctx.enter_context(nc.psum_tensor(name, [P, ROWS], FP32))

        def sem(name):
            return ctx.enter_context(nc.semaphore(name))

        def sems(name, n):
            return [sem(f"{name}{i}") for i in range(n)]

        out0_table = nc.dram_tensor("out0_table", [N, D], FP32, kind="Internal").ap()
        x1eT_spill = nc.dram_tensor("x1eT_spill", [P, GROUPS * ROWS], FP32, kind="Internal").ap()
        mask_dram = nc.dram_tensor("mask_dram", [2, ETILES, P], BF16, kind="Internal").ap()

        ident = sb("ident", [P, P])
        center = sb("center", [P, P])
        raw = sb("raw", [P, 6, P])
        W1A, W1B, EW2, W1R, W2R, RES = range(6)
        wd = sb("wd", [P, P])
        wc1 = sb("wc1", [P, P])
        wc2 = sb("wc2", [P, P])
        wcr = sb("wcr", [P, P])
        wtmp = sb("wtmp", [P, 3, P])
        bias_cols = sb("bias_cols", [P, 3])
        brow = sb("brow", [P, 4, P])
        bpart = sb("bpart", [P, 3, P], BF16)
        bias_rhs = sb("bias_rhs", [P, TILES, P], BF16)
        ones_bf = sb("ones_bf", [P, P], BF16)
        bsum = sb("bsum", [P, 2])
        eps_col = sb("eps_col", [P, 1])
        zeros = sb("zeros", [P, ZERO_CHUNK])

        shared = sb("shared", [P, 6, ROWS])
        index_rows = shared[:, :, :].rearrange("p n d -> p (n d)")[:, 0:20 * P]
        index_rows = index_rows.rearrange("p (a n h e) -> p a n h e", a=2, n=5, h=2)
        idx_in = index_rows[:, 0].bitcast(I32)
        idx_f = index_rows[:, 1]
        same = sb("same", [P, 2, P])
        mask_rows = sb("mask_rows", [P, 2, 2, P], BF16)
        idx = sb("idx", [P, 3, 2 * P], I32)

        x_in = sb("x_in", [P, SLOTS, ROWS])
        x1 = sb("x1", [P, 2, ROWS])
        xT = sb("xT", [P, SLOTS, ROWS])
        hT = sb("hT", [P, 2, ROWS])
        o_rows = sb("o_rows", [P, SLOTS, ROWS])
        bn_a = sb("bn_a", [P, 2, TILES, 6])
        mv_a = sb("mv_a", [P, SLOTS, TILES, 2])
        sd_a = sb("sd_a", [P, SLOTS, TILES])
        rs_a = sb("rs_a", [P, SLOTS, TILES])
        bn_b = sb("bn_b", [P, 2, TILES, 6])
        mv_b = sb("mv_b", [P, SLOTS, TILES, 2])
        sd_b = sb("sd_b", [P, SLOTS, TILES])
        rs_b = sb("rs_b", [P, SLOTS, TILES])

        edge_rows = sb("edge_rows", [P, ETILES * P])
        xs_rows = sb("xs_rows", [P, 2, ROWS])
        xd_rows = sb("xd_rows", [P, 2, ROWS])
        xsT = sb("xsT", [P, 2, ROWS])
        xdT = sb("xdT", [P, 2, ROWS])
        ehT = sb("ehT", [P, 2, ROWS])
        msgT = sb("msgT", [P, 2, ROWS])
        scanT, out0_rows, z_rows = shared[:, 0:2, :], shared[:, 2:4, :], shared[:, 4:6, :]
        x1e_rows = sb("x1e_rows", [P, 2, ROWS])
        x1eT = sb("x1eT", [P, 2, ROWS])
        mask = sb("mask", [P, 2, ROWS], BF16)
        bn_e = sb("bn_e", [P, 2, TILES, 6])
        mv_e = sb("mv_e", [P, 2, TILES, 2])
        sd_e = sb("sd_e", [P, 2, TILES])
        rs_e = sb("rs_e", [P, 2, TILES])
        bn_y = sb("bn_y", [P, 2, TILES, 6])
        mv_y = sb("mv_y", [P, 2, TILES, 2])
        sd_y = sb("sd_y", [P, 2, TILES])
        rs_y = sb("rs_y", [P, 2, TILES])
        zsT_sum = scanT
        sumT = xsT
        eh2T = ehT

        psT = ps("psT")
        psH = ps("psH")
        psY = [ps("psY0"), ps("psY1")]
        psE = [ps(f"psE{i}") for i in range(4)]

        s_w = sem("weights_loaded")
        s_i = sem("indices_loaded")
        s_iz = sem("index_pads_written")
        s_c = sem("constants_built")
        s_c2 = sem("center_built")
        s_dv = sem("setup_vector_steps")
        s_pe = sem("setup_tensor_steps")
        s_mst = sem("masks_stored")
        s_zt = sem("zero_tile_written")
        s_zf = sem("table_cleared")
        x_loaded = sems("x_loaded", SLOTS)
        stored = sems("stored", SLOTS)
        bn1_done = sem("bn1_done")
        var1_done = sem("var1_done")
        std1_done = sem("std1_done")
        rstd1_done = sem("rstd1_done")
        x1_done = sem("x1_done")
        t_done = sem("t_done")
        xT_done = sem("xT_done")
        w1_done = sem("w1_done")
        hT_done = sem("hT_done")
        y_done = sem("y_done")
        bn2_done = sem("bn2_done")
        var2_done = sem("var2_done")
        std2_done = sem("std2_done")
        rstd2_done = sem("rstd2_done")
        o_done = sem("o_done")
        src_gathered = sems("src_gathered", 2)
        xs_copied = sems("xs_copied", 2)
        dst_gathered = sems("dst_gathered", 2)
        mask_loaded = sems("mask_loaded", 2)
        tx_done = sem("tx_done")
        xsdT_done = sem("xsdT_done")
        eh_done = sem("eh_done")
        ehT_done = sem("ehT_done")
        m_done = sem("m_done")
        msg_done = sem("msg_done")
        max_done = sem("max_done")
        bt_done = sem("bt_done")
        out0_done = sem("out0_done")
        z_done = sem("z_done")
        bne_done = sem("bne_done")
        vare_done = sem("vare_done")
        stde_done = sem("stde_done")
        rstde_done = sem("rstde_done")
        x1e_done = sem("x1e_done")
        xt_done = sem("xt_done")
        x1eT_done = sem("x1eT_done")
        spilled = sems("spilled", 2)
        scattered = sems("scattered", 2)
        z_gathered = sems("z_gathered", 2)
        maskb_loaded = sems("maskb_loaded", 2)
        x1eT_loaded = sems("x1eT_loaded", 2)
        bnz_done = sem("bnz_done")
        varz_done = sem("varz_done")
        stdz_done = sem("stdz_done")
        rstdz_done = sem("rstdz_done")
        x1s_done = sem("x1s_done")
        zt_done = sem("zt_done")
        sum_done = sem("sum_done")
        hsum_done = sem("hsum_done")
        we_done = sem("we_done")
        eh2_done = sem("eh2_done")
        ye_done = sem("ye_done")
        bny_done = sem("bny_done")
        vary_done = sem("vary_done")
        stdy_done = sem("stdy_done")
        rstdy_done = sem("rstdy_done")
        res_done = sem("res_done")
        final = sems("final", 2)

        IDX_STEP = 6
        SETUP_STEPS = 21

        def unit(b, k):
            return b + k // SLOTS, k % SLOTS

        def is_unit(b, k):
            return not isinstance(b, int) or 0 <= b * SLOTS + k < UNITS

        def group(i, q):
            return i + q // 2, q % 2

        def is_group(i, q):
            return not isinstance(i, int) or 0 <= 2 * i + q < GROUPS

        def wait(eng, s, n):
            if not isinstance(n, int) or n > 0:
                eng.wait_ge(s, n)

        def tiles(ap):
            return ap.rearrange("p (t d) -> p t d", t=TILES)

        def cut(t):
            return slice(t * P, (t + 1) * P)

        def walk(eng, dense, step_a, tail_a, lead_b, step_b):
            def body(b):
                for k in range(SLOTS):
                    dense(b, k)

            def pair(step, i, b):
                for q in range(2):
                    step(i, q, b, 2 * q)

            body(0)
            with eng.Fori(1, FIRST_A) as b:
                body(b)
            pair(step_a, 0, FIRST_A)
            with eng.Fori(1, PAIRS) as i:
                pair(step_a, i, i + FIRST_A)
            tail_a()
            lead_b()
            pair(step_b, 0, FIRST_B)
            with eng.Fori(1, PAIRS_B1 - 1) as i:
                pair(step_b, i, i + FIRST_B)
            pair(step_b, PAIRS_B1 - 1, LAST)
            for k in range(3):
                dense(LAST + 1, k)
            with eng.Fori(PAIRS_B1, PAIRS - 1) as i:
                pair(step_b, i, None)
            pair(step_b, PAIRS - 1, None)
            pair(step_b, PAIRS, None)

        block = ctx.enter_context(nc.Block())

        @block.sync
        def _(sp):
            sp.wait_ge(s_iz, 1)
            HALF = P * P
            for n, a in enumerate((src, dst, dst)):
                sp.dma_start(idx_in[:, n, 0, :], a[0:HALF].rearrange("(j p) -> j p", p=P)).then_inc(s_i, 16)
                sp.dma_start(idx_in[0:FULL - P, n, 1, :],
                             a[HALF:FULL * P].rearrange("(j p) -> j p", p=P)).then_inc(s_i, 16)
                sp.dma_start(idx_in[FULL - P:FULL - P + 1, n, 1, 0:REST],
                             a[FULL * P:E].rearrange("(j p) -> j p", j=1)).then_inc(s_i, 16)
            sp.dma_start(idx_in[:, 3, 0, :], dst[1:HALF + 1].rearrange("(j p) -> j p", p=P)).then_inc(s_i, 16)
            sp.dma_start(idx_in[0:FULL - P, 3, 1, :],
                         dst[HALF + 1:FULL * P + 1].rearrange("(j p) -> j p", p=P)).then_inc(s_i, 16)
            sp.dma_start(idx_in[FULL - P:FULL - P + 1, 3, 1, 0:REST - 1],
                         dst[FULL * P + 1:E].rearrange("(j p) -> j p", j=1)).then_inc(s_i, 16)
            sp.dma_start(idx_in[0:1, 4, 0, 1:P], dst[0:P - 1].rearrange("(j p) -> j p", j=1)).then_inc(s_i, 16)
            sp.dma_start(idx_in[1:P, 4, 0, :], dst[P - 1:HALF - 1].rearrange("(j p) -> j p", p=P)).then_inc(s_i, 16)
            sp.dma_start(idx_in[0:FULL - P, 4, 1, :],
                         dst[HALF - 1:FULL * P - 1].rearrange("(j p) -> j p", p=P)).then_inc(s_i, 16)
            sp.dma_start(idx_in[FULL - P:FULL - P + 1, 4, 1, 0:REST],
                         dst[FULL * P - 1:E - 1].rearrange("(j p) -> j p", j=1)).then_inc(s_i, 16)

            def number(n, top):
                return n if isinstance(n, int) else sp.snap(n, min_val=-1, max_val=top)

            def rows_of(a, b, k):
                base = (b * SLOTS + k) * ROWS
                base = min(base, N - ROWS) if isinstance(b, int) else number(base, N - ROWS)
                return a[bass.ds(base, ROWS), :].rearrange("(p r) d -> p (r d)", p=P)

            def load(b, k):
                b, k = unit(b, k)
                if is_unit(b, k):
                    rows = rows_of(x, b, k)
                    wait(sp, x1_done, (b - 1) * SLOTS + k + 1)
                    sp.dma_start(x_in[:, k, :], rows).then_inc(x_loaded[k], 16)

            def store(b, k):
                b, k = unit(b, k)
                if is_unit(b, k):
                    rows = rows_of(out, b, k)
                    wait(sp, o_done, b * SLOTS + k + 1)
                    if isinstance(b, int) and b * SLOTS + k == UNITS - 1:
                        sp.wait_ge(stored[(k - 1) % SLOTS], 16 * (b + (k - 1) // SLOTS + 1))
                    sp.dma_start(rows, o_rows[:, k, :]).then_inc(stored[k], 16)

            def dense(b, k):
                load(b, k + 3)
                store(b, k - 4)
                if isinstance(b, int) and b * SLOTS + k == UNITS + 2:
                    store(b, -1)

            def feed_a(i, q):
                i, q = group(i, q)
                if not is_group(i, q):
                    return
                g = 2 * i + q
                at = number(g * ROWS, (GROUPS - 1) * ROWS)
                wait(sp, tx_done, g - 1)
                wait(sp, max_done, g - 1)
                wait(sp, src_gathered[q], 16 * TILES * (i + 1))
                sp.dma_start(xs_rows[:, q, :], edge_rows[:, bass.ds(at, ROWS)]).then_inc(xs_copied[q], 16)
                sp.dma_start(mask[:, q, :], mask_dram[0].rearrange("t e -> (t e)")[bass.ds(at, ROWS)]
                             .unsqueeze(0).broadcast_to([P, ROWS])).then_inc(mask_loaded[q], 16)

            def spill(i, q):
                i, q = group(i, q)
                if is_group(i, q):
                    g = 2 * i + q
                    at = number(g * ROWS, (GROUPS - 1) * ROWS)
                    wait(sp, x1eT_done, g + 1)
                    sp.dma_start(x1eT_spill[:, bass.ds(at, ROWS)], x1eT[:, q, :]).then_inc(spilled[q], 16)

            def step_a(i, q, b, k):
                dense(b, k)
                spill(i, q - 2)
                feed_a(i, q)
                dense(b, k + 1)

            def tail_a():
                spill(PAIRS - 1, 0)
                spill(PAIRS - 1, 1)
                sp.wait_ge(spilled[0], 16 * PAIRS)
                sp.wait_ge(spilled[1], 16 * PAIRS)

            def feed_b(i, q):
                if is_group(i, q):
                    g = 2 * i + q
                    at = number(g * ROWS, (GROUPS - 1) * ROWS)
                    wait(sp, sum_done, g - 1)
                    wait(sp, ye_done, g - 1)
                    sp.dma_start(mask[:, q, :], mask_dram[1].rearrange("t e -> (t e)")[bass.ds(at, ROWS)]
                                 .unsqueeze(0).broadcast_to([P, ROWS])).then_inc(maskb_loaded[q], 16)
                    sp.dma_start(x1eT[:, q, :], x1eT_spill[:, bass.ds(at, ROWS)]).then_inc(x1eT_loaded[q], 16)

            def step_b(i, q, b, k):
                if b is not None:
                    dense(b, k)
                feed_b(i, q)
                if b is not None:
                    dense(b, k + 1)

            sp.wait_ge(s_mst, 64)
            for k in range(3):
                load(0, k)
            walk(sp, dense, step_a, tail_a, lambda: sp.wait_ge(max_done, GROUPS), step_b)
            for k in range(SLOTS):
                sp.wait_ge(stored[k], 16 * BODIES)

        @block.gpsimd
        def _(pool):
            nc.gpsimd.memset(idx_in[:, 0:2, :, :], 0)
            nc.gpsimd.memset(idx_in[:, 2, :, :], BIG)
            nc.gpsimd.memset(idx_in[:, 3:5, :, :], -1).then_inc(s_iz, 1)
            nc.gpsimd.memset(ident[:, :], 0.0)
            nc.gpsimd.memset(center[:, :], -1.0 / P).then_inc(s_c2, 1)
            pool.wait_ge(s_c2, 1)
            nc.gpsimd.affine_select(out=ident[:, :], in_=ident[:, :], compare_op=ALU.not_equal, fill=1.0,
                                    base=0, pattern=[[-1, P]], channel_multiplier=1)
            nc.gpsimd.affine_select(out=center[:, :], in_=center[:, :], compare_op=ALU.not_equal, fill=1.0 - 1.0 / P,
                                    base=0, pattern=[[-1, P]], channel_multiplier=1).then_inc(s_c, 1)
            pool.wait_ge(s_dv, IDX_STEP)
            SRC, DST, SCAT = range(3)

            def gather(to, table, what, t, done, add=False):
                kw = dict(compute_op=ALU.add) if add else {}
                nc.gpsimd.indirect_dma_start(to, None, table, bass.IndirectOffsetOnAxis(idx[:, what, t:t + 1], 0),
                                             bounds_check=N - 1, oob_is_err=True, **kw).then_inc(done, 16)

            def scatter(table, frm, t, done):
                nc.gpsimd.indirect_dma_start(table, bass.IndirectOffsetOnAxis(idx[:, SCAT, t:t + 1], 0), frm, None,
                                             bounds_check=N - 1, oob_is_err=False).then_inc(done, 16)

            for g in range(GROUPS):
                i, q = divmod(g, 2)
                wait(pool, src_gathered[q], 16 * TILES * i)
                for t in range(TILES):
                    gather(edge_rows[:, cut(g * TILES + t)], x, SRC, g * TILES + t, src_gathered[q])

            def gather_dst(g):
                i, q = divmod(g, 2)
                wait(pool, dst_gathered[q], 16 * TILES * i)
                wait(pool, z_done, g - 1)
                for t in range(TILES):
                    gather(xd_rows[:, q, cut(t)], x, DST, g * TILES + t, dst_gathered[q])

            gather_dst(0)
            gather_dst(1)
            pool.wait_ge(s_zf, 16 * ZCH)
            for g in range(GROUPS):
                i, q = divmod(g, 2)
                pool.wait_ge(out0_done, g + 1)
                wait(pool, scattered[q], 16 * TILES * i)
                for t in range(TILES):
                    scatter(out0_table, out0_rows[:, q, cut(t)], g * TILES + t, scattered[q])
                if g + 2 < GROUPS:
                    gather_dst(g + 2)

            for q in range(2):
                pool.wait_ge(scattered[q], 16 * TILES * PAIRS)
                pool.wait_ge(xs_copied[q], 16 * PAIRS)
            for g in range(GROUPS):
                i, q = divmod(g, 2)
                wait(pool, z_gathered[q], 16 * TILES * i)
                for t in range(TILES):
                    gather(edge_rows[:, cut(g * TILES + t)], out0_table, SRC, g * TILES + t, z_gathered[q], add=True)

            for k in range(SLOTS):
                pool.wait_ge(stored[k], 16 * BODIES)
            for g in range(GROUPS):
                i, q = divmod(g, 2)
                pool.wait_ge(res_done, g + 1)
                wait(pool, final[q], 16 * TILES * i)
                for t in range(TILES):
                    scatter(out, edge_rows[:, cut(g * TILES + t)], g * TILES + t, final[q])
            for q in range(2):
                pool.wait_ge(final[q], 16 * TILES * PAIRS)

        @block.vector
        def _(dve):
            v = nc.vector
            step = [0]

            def link(ins):
                step[0] += 1
                ins.then_inc(s_dv, 1)
                dve.wait_ge(s_dv, step[0])

            v.memset(zeros[:, :], 0.0).then_inc(s_zt, 1)
            v.memset(eps_col[:, :], EPS)
            v.memset(ones_bf[:, :], 1.0)
            dve.wait_ge(s_i, 16 * 16)
            link(v.tensor_copy(idx_f[:, :, :, :], idx_in[:, :, :, :]))
            link(v.tensor_tensor(same[:, :, :], idx_f[:, 1, :, :], idx_f[:, 3, :, :], ALU.is_equal))
            link(v.scalar_tensor_tensor(out=idx_f[:, 2, :, :], in0=same[:, :, :], scalar=float(BIG),
                                        in1=idx_f[:, 2, :, :], op0=ALU.mult, op1=ALU.add))
            link(v.tensor_tensor(same[:, :, :], idx_f[:, 1, :, :], idx_f[:, 4, :, :], ALU.is_equal))
            v.tensor_scalar(mask_rows[:, 0, :, :], same[:, :, :], 1.0, -LOWEST, ALU.subtract, ALU.mult)
            link(v.tensor_copy(mask_rows[:, 1, :, :], same[:, :, :]))
            dve.wait_ge(s_pe, 1)
            v.tensor_copy(idx[:, 0, :], psE[0][:, 0:2 * P])
            v.tensor_copy(idx[:, 1, :], psE[0][:, 2 * P:4 * P])
            link(v.tensor_copy(idx[:, 2, :], psE[1][:, 0:2 * P]))
            dve.wait_ge(s_w, 16 * 11)
            dve.wait_ge(s_c, 1)
            v.tensor_tensor(wd[:, :], raw[:, W1A, :], raw[:, W1B, :], ALU.subtract)
            link(v.tensor_tensor(wtmp[:, 0, :], raw[:, RES, :], ident[:, :], ALU.add))
            dve.wait_ge(s_pe, 2)
            v.tensor_copy(wc1[:, :], psE[2][:, 0:P])
            link(v.tensor_copy(wtmp[:, 1:3, :], psE[2][:, P:3 * P].rearrange("p (a b) -> p a b", a=2)))
            dve.wait_ge(s_pe, 3)
            v.tensor_copy(wcr[:, :], psE[3][:, 0:P])
            v.tensor_copy(wc2[:, :], psE[3][:, P:2 * P])
            link(v.tensor_tensor(brow[:, 2, :], brow[:, 0, :], brow[:, 1, :], ALU.add))
            link(v.reduce_sum(bsum[:, 0:1], brow[:, 2, :], axis=AX.X))
            link(v.tensor_scalar(bsum[:, 1:2], bsum[:, 0:1], 1.0 / P, None, ALU.mult))
            link(v.tensor_scalar(brow[:, 2, :], brow[:, 2, :], bsum[:, 1:2], None, ALU.subtract))
            link(v.tensor_copy(bpart[:, 0, :], brow[:, 2, :]))
            link(v.tensor_tensor(brow[:, 3, :], brow[:, 2, :], bpart[:, 0, :], ALU.subtract))
            link(v.tensor_copy(bpart[:, 1, :], brow[:, 3, :]))
            link(v.tensor_tensor(brow[:, 2, :], brow[:, 3, :], bpart[:, 1, :], ALU.subtract))
            link(v.tensor_copy(bpart[:, 2, :], brow[:, 2, :]))
            link(v.tensor_scalar(brow[:, 0, :], bpart[:, 0, :], ident[:, 0:1], None, ALU.mult))
            for n in (1, 2):
                link(v.scalar_tensor_tensor(out=brow[:, n % 2, :], in0=bpart[:, n, :], scalar=ident[:, n:n + 1],
                                            in1=brow[:, (n + 1) % 2, :], op0=ALU.mult, op1=ALU.add))
            for t in range(TILES):
                last = v.tensor_copy(bias_rhs[:, t, :], brow[:, 0, :])
            link(last)
            assert step[0] == SETUP_STEPS

            def stats(bn, rows, done):
                for t in range(TILES):
                    last = v.bn_stats(bn[:, t, :], rows[:, cut(t)])
                last.then_inc(done, 1)

            def aggregate(mv, bn, done):
                for t in range(TILES):
                    last = v.bn_aggr(mv[:, t, :], bn[:, t, :])
                last.then_inc(done, 1)

            def scale(to, rows, rs, done):
                v.tensor_tensor(tiles(to), tiles(rows), rs.unsqueeze(2).broadcast_to([P, TILES, P]),
                                ALU.mult).then_inc(done, 1)

            def norm1_stats(b, k):
                b, k = unit(b, k)
                if is_unit(b, k):
                    dve.wait_ge(x_loaded[k], 16 * (b + 1))
                    stats(bn_a[:, k % 2, :, :], x_in[:, k, :], bn1_done)

            def norm1_ready(b, k):
                b, k = unit(b, k)
                if is_unit(b, k):
                    dve.wait_ge(bn1_done, b * SLOTS + k + 1)

            def norm1_var(b, k):
                b, k = unit(b, k)
                if is_unit(b, k):
                    aggregate(mv_a[:, k, :, :], bn_a[:, k % 2, :, :], var1_done)

            def norm1_recip(b, k):
                b, k = unit(b, k)
                if is_unit(b, k):
                    dve.wait_ge(std1_done, b * SLOTS + k + 1)
                    v.reciprocal(rs_a[:, k, :], sd_a[:, k, :]).then_inc(rstd1_done, 1)

            def norm1_scale(b, k):
                b, k = unit(b, k)
                if is_unit(b, k):
                    n = b * SLOTS + k
                    dve.wait_ge(rstd1_done, n + 1)
                    wait(dve, t_done, n - 1)
                    scale(x1[:, k % 2, :], x_in[:, k, :], rs_a[:, k, :], x1_done)

            def norm2_stats(b, k):
                b, k = unit(b, k)
                if is_unit(b, k):
                    dve.wait_ge(y_done, b * SLOTS + k + 1)
                    stats(bn_b[:, k % 2, :, :], psY[k % 2], bn2_done)

            def norm2_ready(b, k):
                b, k = unit(b, k)
                if is_unit(b, k):
                    dve.wait_ge(bn2_done, b * SLOTS + k + 1)

            def norm2_var(b, k):
                b, k = unit(b, k)
                if is_unit(b, k):
                    aggregate(mv_b[:, k, :, :], bn_b[:, k % 2, :, :], var2_done)

            def norm2_recip(b, k):
                b, k = unit(b, k)
                if is_unit(b, k):
                    dve.wait_ge(std2_done, b * SLOTS + k + 1)
                    v.reciprocal(rs_b[:, k, :], sd_b[:, k, :]).then_inc(rstd2_done, 1)

            def dense(b, k):
                norm2_stats(b, k - 3)
                dense_rest(b, k)

            def dense_rest(b, k):
                norm2_ready(b, k - 3)
                norm1_recip(b, k + 1)
                norm2_var(b, k - 3)
                norm1_scale(b, k + 1)
                norm1_stats(b, k + 2)
                norm1_ready(b, k + 2)
                norm2_recip(b, k - 3)
                norm1_var(b, k + 2)

            def residual0(i, q):
                i, q = group(i, q)
                if is_group(i, q):
                    g = 2 * i + q
                    dve.wait_ge(out0_done, g + 1)
                    wait(dve, x1e_done, g - 1)
                    v.tensor_tensor(z_rows[:, q, :], out0_rows[:, q, :], xd_rows[:, q, :], ALU.add).then_inc(z_done, 1)
                    dve.wait_ge(z_done, g + 1)
                    stats(bn_e[:, q, :, :], z_rows[:, q, :], bne_done)

            def residual0_ready(i, q):
                i, q = group(i, q)
                if is_group(i, q):
                    dve.wait_ge(bne_done, 2 * i + q + 1)

            def residual0_var(i, q):
                i, q = group(i, q)
                if is_group(i, q):
                    aggregate(mv_e[:, q, :, :], bn_e[:, q, :, :], vare_done)

            def scale0(i, q):
                i, q = group(i, q)
                if is_group(i, q):
                    g = 2 * i + q
                    dve.wait_ge(stde_done, g + 1)
                    v.reciprocal(rs_e[:, q, :], sd_e[:, q, :]).then_inc(rstde_done, 1)
                    dve.wait_ge(rstde_done, g + 1)
                    wait(dve, xt_done, g - 1)
                    scale(x1e_rows[:, q, :], z_rows[:, q, :], rs_e[:, q, :], x1e_done)

            def segment_max(i, q):
                if is_group(i, q):
                    g = 2 * i + q
                    first = isinstance(i, int) and g == 0
                    dve.wait_ge(mask_loaded[q], 16 * (i + 1))
                    dve.wait_ge(msg_done, g + 1)
                    wait(dve, bt_done, g - 1)
                    wait(dve, max_done, g)
                    v.tensor_tensor_scan(scanT[:, q, :], mask[:, q, :], msgT[:, q, :],
                                         0.0 if first else scanT[:, 1 - q, ROWS - 1:ROWS],
                                         ALU.add, ALU.max).then_inc(max_done, 1)

            def step_a(i, q, b, k):
                dense(b, k)
                residual0(i, q - 1)
                residual0_ready(i, q - 1)
                norm2_stats(b, k - 2)
                residual0_var(i, q - 1)
                dense_rest(b, k + 1)
                scale0(i, q - 1)
                segment_max(i, q)

            def tail_a():
                residual0(PAIRS, -1)
                residual0_ready(PAIRS, -1)
                residual0_var(PAIRS, -1)
                scale0(PAIRS, -1)

            def src_stats(i, q):
                i, q = group(i, q)
                if is_group(i, q):
                    dve.wait_ge(z_gathered[q], 16 * TILES * (i + 1))
                    g = 2 * i + q
                    for t in range(TILES):
                        last = v.bn_stats(bn_e[:, q, t, :], edge_rows[:, bass.ds(g * ROWS + t * P, P)])
                    last.then_inc(bnz_done, 1)

            def src_ready(i, q):
                i, q = group(i, q)
                if is_group(i, q):
                    dve.wait_ge(bnz_done, 2 * i + q + 1)

            def src_var(i, q):
                i, q = group(i, q)
                if is_group(i, q):
                    aggregate(mv_e[:, q, :, :], bn_e[:, q, :, :], varz_done)

            def src_recip(i, q):
                i, q = group(i, q)
                if is_group(i, q):
                    dve.wait_ge(stdz_done, 2 * i + q + 1)
                    v.reciprocal(rs_e[:, q, :], sd_e[:, q, :]).then_inc(rstdz_done, 1)

            def src_scale(i, q):
                i, q = group(i, q)
                if is_group(i, q):
                    g = 2 * i + q
                    dve.wait_ge(rstdz_done, g + 1)
                    wait(dve, zt_done, g - 1)
                    scale(x1e_rows[:, q, :], edge_rows[:, bass.ds(g * ROWS, ROWS)], rs_e[:, q, :], x1s_done)

            def segment_sum(i, q):
                if is_group(i, q):
                    g = 2 * i + q
                    first = isinstance(i, int) and g == 0
                    dve.wait_ge(maskb_loaded[q], 16 * (i + 1))
                    dve.wait_ge(zt_done, g + 1)
                    wait(dve, sum_done, g)
                    v.tensor_tensor_scan(zsT_sum[:, q, :], mask[:, q, :], psE[0][:, :],
                                         0.0 if first else zsT_sum[:, 1 - q, ROWS - 1:ROWS],
                                         ALU.mult, ALU.add).then_inc(sum_done, 1)

            def add_dst(i, q):
                if is_group(i, q):
                    g = 2 * i + q
                    dve.wait_ge(x1eT_loaded[q], 16 * (i + 1))
                    dve.wait_ge(sum_done, g + 1)
                    wait(dve, we_done, g - 1)
                    v.tensor_tensor(sumT[:, q, :], zsT_sum[:, q, :], x1eT[:, q, :], ALU.add).then_inc(hsum_done, 1)

            def out_stats(i, q):
                i, q = group(i, q)
                if is_group(i, q):
                    dve.wait_ge(ye_done, 2 * i + q + 1)
                    stats(bn_y[:, q, :, :], psE[2 + q], bny_done)

            def out_ready(i, q):
                i, q = group(i, q)
                if is_group(i, q):
                    dve.wait_ge(bny_done, 2 * i + q + 1)

            def out_var(i, q):
                i, q = group(i, q)
                if is_group(i, q):
                    aggregate(mv_y[:, q, :, :], bn_y[:, q, :, :], vary_done)

            def out_recip(i, q):
                i, q = group(i, q)
                if is_group(i, q):
                    dve.wait_ge(stdy_done, 2 * i + q + 1)
                    v.reciprocal(rs_y[:, q, :], sd_y[:, q, :]).then_inc(rstdy_done, 1)

            def lead_b():
                src_stats(0, 0)
                src_ready(0, 0)
                src_var(0, 0)
                src_stats(0, 1)
                src_ready(0, 1)
                src_recip(0, 0)
                src_var(0, 1)
                src_scale(0, 0)

            def step_b(i, q, b, k):
                if b is not None:
                    dense(b, k)
                out_stats(i, q - 2)
                out_ready(i, q - 2)
                src_recip(i, q + 1)
                out_var(i, q - 2)
                src_scale(i, q + 1)
                segment_sum(i, q)
                src_stats(i, q + 2)
                add_dst(i, q)
                src_ready(i, q + 2)
                out_recip(i, q - 2)
                src_var(i, q + 2)
                if b is not None:
                    dense(b, k + 1)

            norm1_stats(0, 0)
            norm1_ready(0, 0)
            norm1_var(0, 0)
            norm1_stats(0, 1)
            norm1_ready(0, 1)
            norm1_recip(0, 0)
            norm1_var(0, 1)
            norm1_scale(0, 0)
            walk(dve, dense, step_a, tail_a, lead_b, step_b)

        @block.scalar
        def _(act):
            a = nc.scalar
            for n, w in enumerate((e_w1[0:P, :], e_w1[P:2 * P, :], e_w2, w1, w2, wres)):
                act.dma_start(raw[:, n, :], w).then_inc(s_w, 16)
            for n, c in enumerate((e_b1, e_b2, b1)):
                act.dma_start(bias_cols[:, n:n + 1], c.rearrange("(p o) -> p o", o=1)).then_inc(s_w, 16)
            for n, r in enumerate((b2, bres)):
                act.dma_start(brow[:, n, :], r.unsqueeze(0).broadcast_to([P, P])).then_inc(s_w, 16)
            act.wait_ge(s_dv, 5)
            for m in range(2):
                for h in range(2):
                    n = P if h == 0 else ETILES - P
                    act.dma_start(mask_dram[m, h * P:h * P + n, :], mask_rows[0:n, m, h, :]).then_inc(s_mst, 16)
            act.wait_ge(s_zt, 1)
            table = out0_table.rearrange("n d -> (n d)").rearrange("(p f) -> p f", p=P)
            with act.Fori(0, ZCH) as c:
                act.dma_start(table[:, bass.ds(c * ZERO_CHUNK, ZERO_CHUNK)], zeros[:, :]).then_inc(s_zf, 16)
            act.wait_ge(s_w, 16 * 11)
            act.wait_ge(s_dv, SETUP_STEPS)

            def relu(b, k):
                b, k = unit(b, k)
                if is_unit(b, k):
                    n = b * SLOTS + k
                    act.wait_ge(w1_done, n + 1)
                    wait(act, y_done, n - 1)
                    a.activation(hT[:, k % 2, :], psH[:, :], ACT.Relu, bias=bias_cols[:, 2:3]).then_inc(hT_done, 1)

            def copy_xT(b, k):
                b, k = unit(b, k)
                if is_unit(b, k):
                    n = b * SLOTS + k
                    act.wait_ge(t_done, n + 1)
                    wait(act, y_done, n - 3)
                    a.copy(xT[:, k, :], psT[:, :]).then_inc(xT_done, 1)

            def root(sd, mv, done):
                a.activation(sd, mv[:, :, 1], ACT.Sqrt, bias=eps_col[:, 0:1]).then_inc(done, 1)

            def root1(b, k):
                b, k = unit(b, k)
                if is_unit(b, k):
                    act.wait_ge(var1_done, b * SLOTS + k + 1)
                    root(sd_a[:, k, :], mv_a[:, k, :, :], std1_done)

            def root2(b, k):
                b, k = unit(b, k)
                if is_unit(b, k):
                    act.wait_ge(var2_done, b * SLOTS + k + 1)
                    root(sd_b[:, k, :], mv_b[:, k, :, :], std2_done)

            def finish(b, k):
                b, k = unit(b, k)
                if is_unit(b, k):
                    act.wait_ge(rstd2_done, b * SLOTS + k + 1)
                    wait(act, stored[k], 16 * b)
                    for t in range(TILES):
                        last = a.activation(o_rows[:, k, cut(t)], psY[k % 2][:, cut(t)], ACT.Copy,
                                            scale=rs_b[:, k, t:t + 1])
                    last.then_inc(o_done, 1)

            def first_half(b, k):
                relu(b, k - 1)
                copy_xT(b, k)

            def second_half(b, k):
                root2(b, k - 3)
                finish(b, k - 3)
                root1(b, k + 2)

            def dense(b, k):
                first_half(b, k)
                second_half(b, k)

            def copy_xsd(i, q):
                g = 2 * i + q
                act.wait_ge(tx_done, g + 1)
                wait(act, eh_done, g - 1)
                a.copy(xsT[:, q, :], psE[0][:, :])
                a.copy(xdT[:, q, :], psE[1][:, :]).then_inc(xsdT_done, 1)

            def relu0(i, q):
                g = 2 * i + q
                act.wait_ge(eh_done, g + 1)
                wait(act, m_done, g - 1)
                a.activation(ehT[:, q, :], psE[2][:, :], ACT.Relu, bias=bias_cols[:, 0:1]).then_inc(ehT_done, 1)

            def message(i, q):
                g = 2 * i + q
                act.wait_ge(m_done, g + 1)
                wait(act, max_done, g - 1)
                a.activation(msgT[:, q, :], psE[0][:, :], ACT.Identity, bias=bias_cols[:, 1:2]).then_inc(msg_done, 1)

            def copy_out0(i, q):
                i, q = group(i, q)
                if is_group(i, q):
                    act.wait_ge(bt_done, 2 * i + q + 1)
                    wait(act, scattered[q], 16 * TILES * i)
                    wait(act, z_done, 2 * i + q - 1)
                    a.copy(out0_rows[:, q, :], psE[3][:, :]).then_inc(out0_done, 1)

            def root0(i, q):
                i, q = group(i, q)
                if is_group(i, q):
                    act.wait_ge(vare_done, 2 * i + q + 1)
                    root(sd_e[:, q, :], mv_e[:, q, :, :], stde_done)

            def copy_x1eT(i, q):
                i, q = group(i, q)
                if is_group(i, q):
                    act.wait_ge(xt_done, 2 * i + q + 1)
                    wait(act, spilled[q], 16 * i)
                    a.copy(x1eT[:, q, :], psE[1][:, :]).then_inc(x1eT_done, 1)

            def step_a(i, q, b, k):
                first_half(b, k)
                copy_xsd(i, q)
                second_half(b, k)
                copy_out0(i, q - 1)
                first_half(b, k + 1)
                relu0(i, q)
                root0(i, q - 1)
                second_half(b, k + 1)
                message(i, q)
                copy_x1eT(i, q - 1)

            def tail_a():
                copy_out0(PAIRS, -1)
                root0(PAIRS, -1)
                copy_x1eT(PAIRS, -1)

            def root_src(i, q):
                i, q = group(i, q)
                if is_group(i, q):
                    act.wait_ge(varz_done, 2 * i + q + 1)
                    root(sd_e[:, q, :], mv_e[:, q, :, :], stdz_done)

            def relu1(i, q):
                i, q = group(i, q)
                if is_group(i, q):
                    g = 2 * i + q
                    act.wait_ge(we_done, g + 1)
                    wait(act, ye_done, g - 1)
                    a.activation(eh2T[:, q, :], psE[1][:, :], ACT.Relu, bias=bias_cols[:, 2:3]).then_inc(eh2_done, 1)

            def root_out(i, q):
                i, q = group(i, q)
                if is_group(i, q):
                    act.wait_ge(vary_done, 2 * i + q + 1)
                    root(sd_y[:, q, :], mv_y[:, q, :, :], stdy_done)

            def finish1(i, q):
                i, q = group(i, q)
                if is_group(i, q):
                    g = 2 * i + q
                    act.wait_ge(rstdy_done, g + 1)
                    for t in range(TILES):
                        last = a.activation(edge_rows[:, bass.ds(g * ROWS + t * P, P)], psE[2 + q][:, cut(t)],
                                            ACT.Copy, scale=rs_y[:, q, t:t + 1])
                    last.then_inc(res_done, 1)

            def lead_b():
                root_src(0, 0)
                root_src(0, 1)

            def step_b(i, q, b, k):
                if b is not None:
                    dense(b, k)
                relu1(i, q - 1)
                root_out(i, q - 2)
                finish1(i, q - 2)
                root_src(i, q + 2)
                if b is not None:
                    dense(b, k + 1)

            root1(0, 0)
            root1(0, 1)
            walk(act, dense, step_a, tail_a, lead_b, step_b)

        @block.tensor
        def _(pe):
            t_ = nc.tensor
            pe.wait_ge(s_c, 1)
            pe.wait_ge(s_dv, 3)
            for n in range(3):
                for h in range(2):
                    at = 2 * n + h
                    last = t_.transpose(psE[at // 4][:, cut(at % 4)], idx_f[:, n, h, :], ident[:, :])
            last.then_inc(s_pe, 1)
            pe.wait_ge(s_w, 16 * 11)
            pe.wait_ge(s_dv, 7)
            t_.matmul(psE[2][:, 0:P], center[:, :], raw[:, W1R, :], start=True, stop=True)
            t_.matmul(psE[2][:, P:2 * P], wtmp[:, 0, :], center[:, :], start=True, stop=True)
            t_.transpose(psE[2][:, 2 * P:3 * P], raw[:, W2R, :], ident[:, :]).then_inc(s_pe, 1)
            pe.wait_ge(s_dv, 8)
            t_.matmul(psE[3][:, 0:P], wtmp[:, 1, :], center[:, :], start=True, stop=True)
            t_.matmul(psE[3][:, P:2 * P], wtmp[:, 2, :], center[:, :], start=True, stop=True).then_inc(s_pe, 1)
            pe.wait_ge(s_dv, SETUP_STEPS)

            def transpose4(to, rows, done=None):
                for t in range(TILES):
                    last = t_.transpose(to[:, cut(t)], rows[:, cut(t)], ident[:, :])
                if done is not None:
                    last.then_inc(done, 1)

            def product_rows(to, h, xt, done):
                t_.matmul(to[:, :], ones_bf[:, :], bias_rhs[:, :, :].rearrange("p t d -> p (t d)"),
                          start=True, stop=False, skip_group_check=True)
                for t in range(TILES):
                    t_.matmul(to[:, cut(t)], h[:, cut(t)], wc2[:, :], start=False, stop=False, skip_group_check=True)
                    last = t_.matmul(to[:, cut(t)], xt[:, cut(t)], wcr[:, :], start=False, stop=t == TILES - 1,
                                     skip_group_check=True)
                last.then_inc(done, 1)

            def first_product(b, k):
                b, k = unit(b, k)
                if is_unit(b, k):
                    n = b * SLOTS + k
                    pe.wait_ge(xT_done, n + 1)
                    wait(pe, hT_done, n)
                    t_.matmul(psH[:, :], wc1[:, :], xT[:, k, :], start=True, stop=True).then_inc(w1_done, 1)

            def transposed(b, k):
                b, k = unit(b, k)
                if is_unit(b, k):
                    n = b * SLOTS + k
                    pe.wait_ge(x1_done, n + 1)
                    wait(pe, xT_done, n)
                    transpose4(psT, x1[:, k % 2, :], t_done)

            def second_product(b, k):
                b, k = unit(b, k)
                if is_unit(b, k):
                    n = b * SLOTS + k
                    pe.wait_ge(hT_done, n + 1)
                    wait(pe, o_done, n - 1)
                    product_rows(psY[k % 2], hT[:, k % 2, :], xT[:, k, :], y_done)

            def first_half(b, k):
                first_product(b, k - 1)
                transposed(b, k)

            def dense(b, k):
                first_half(b, k)
                second_product(b, k - 2)

            def transpose_in(i, q):
                g = 2 * i + q
                pe.wait_ge(xs_copied[q], 16 * (i + 1))
                pe.wait_ge(dst_gathered[q], 16 * TILES * (i + 1))
                wait(pe, msg_done, g)
                wait(pe, x1eT_done, g - 1)
                transpose4(psE[0], xs_rows[:, q, :])
                transpose4(psE[1], xd_rows[:, q, :], tx_done)

            def edge_product1(i, q):
                g = 2 * i + q
                pe.wait_ge(xsdT_done, g + 1)
                wait(pe, ehT_done, g)
                t_.matmul(psE[2][:, :], wd[:, :], xdT[:, q, :], start=True, stop=False)
                t_.matmul(psE[2][:, :], raw[:, W1B, :], xsT[:, q, :], start=False, stop=True).then_inc(eh_done, 1)

            def edge_product2(i, q):
                g = 2 * i + q
                pe.wait_ge(ehT_done, g + 1)
                t_.matmul(psE[0][:, :], raw[:, EW2, :], ehT[:, q, :], start=True, stop=True).then_inc(m_done, 1)

            def transpose_max(i, q):
                i, q = group(i, q)
                if is_group(i, q):
                    g = 2 * i + q
                    pe.wait_ge(max_done, g + 1)
                    wait(pe, out0_done, g)
                    transpose4(psE[3], scanT[:, q, :], bt_done)

            def transpose_x1e(i, q):
                i, q = group(i, q)
                if is_group(i, q):
                    g = 2 * i + q
                    pe.wait_ge(x1e_done, g + 1)
                    wait(pe, x1eT_done, g)
                    transpose4(psE[1], x1e_rows[:, q, :], xt_done)

            def step_a(i, q, b, k):
                first_half(b, k)
                transpose_in(i, q)
                second_product(b, k - 2)
                transpose_max(i, q - 1)
                first_half(b, k + 1)
                edge_product1(i, q)
                second_product(b, k - 1)
                edge_product2(i, q)
                transpose_x1e(i, q - 1)

            def tail_a():
                transpose_max(PAIRS, -1)
                transpose_x1e(PAIRS, -1)
                pe.wait_ge(x1eT_done, GROUPS)
                pe.wait_ge(msg_done, GROUPS)

            def transpose_src(i, q):
                if is_group(i, q):
                    g = 2 * i + q
                    pe.wait_ge(x1s_done, g + 1)
                    wait(pe, sum_done, g)
                    transpose4(psE[0], x1e_rows[:, q, :], zt_done)

            def edge_product3(i, q):
                i, q = group(i, q)
                if is_group(i, q):
                    g = 2 * i + q
                    pe.wait_ge(hsum_done, g + 1)
                    wait(pe, eh2_done, g)
                    t_.matmul(psE[1][:, :], wc1[:, :], sumT[:, q, :], start=True, stop=True).then_inc(we_done, 1)

            def edge_product4(i, q):
                i, q = group(i, q)
                if is_group(i, q):
                    g = 2 * i + q
                    pe.wait_ge(eh2_done, g + 1)
                    wait(pe, res_done, g - 1)
                    product_rows(psE[2 + q], eh2T[:, q, :], x1eT[:, q, :], ye_done)

            def step_b(i, q, b, k):
                if b is not None:
                    first_half(b, k)
                edge_product3(i, q - 1)
                if b is not None:
                    second_product(b, k - 2)
                transpose_src(i, q)
                if b is not None:
                    dense(b, k + 1)
                edge_product4(i, q - 1)

            walk(pe, dense, step_a, tail_a, lambda: None, step_b)


_INS = ["x", "src", "dst", "L0_gnn_W1", "L0_gnn_b1", "L0_gnn_W2", "L0_gnn_b2", "L1_gnn_W1", "L1_gnn_b1",
        "L1_gnn_W2", "L1_gnn_b2", "L1_gnn_Wres", "L1_gnn_bres"]


def kernel(**inputs):
    import numpy as np
    import concourse.bacc as bacc
    from concourse.bass_utils import run_bass_kernel_spmd

    nc = bacc.Bacc("TRN2", target_bir_lowering=False, num_devices=1)
    arrays, args = {}, []
    for name in _INS:
        a = np.ascontiguousarray(inputs[name])
        arrays[f"in_{name}"] = a
        args.append(nc.dram_tensor(f"in_{name}", a.shape, mybir.dt.from_np(a.dtype), kind="ExternalInput").ap())
    shape = inputs["x"].shape
    args.append(nc.dram_tensor("out_0", shape, FP32, kind="ExternalOutput").ap())
    gnn_program(nc, *args)
    r = run_bass_kernel_spmd(nc, [arrays], core_ids=[0])
    return r.results[0]["out_0"]
```

```python
from contextlib import ExitStack

import concourse.bass as bass
from concourse import mybir

FP32 = mybir.dt.float32
BF16 = mybir.dt.bfloat16
I32 = mybir.dt.int32
ALU = mybir.AluOpType
ACT = mybir.ActivationFunctionType
AX = mybir.AxisListType

P = 128
EPS = 1e-5
TILES = 4
ROWS = TILES * P
SLOTS = 4
BIG = 1 << 21
LOWEST = -3.0e38
EARLY_CLEARS = 8
BODIES_0 = 20


def gnn_program(nc, x, src, dst, e_w1, e_b1, e_w2, e_b2, w1, b1, w2, b2, wres, bres, out):
    N, D = x.shape
    E = src.shape[0]
    UNITS = -(-N // ROWS)
    BODIES = UNITS // SLOTS
    assert UNITS == BODIES * SLOTS and N % 32 == 0
    GROUPS = 2 * -(-E // (2 * ROWS))
    PAIRS = GROUPS // 2
    ETILES = GROUPS * TILES
    FULL = E // P
    REST = E - FULL * P
    assert GROUPS % SLOTS == 2
    QUADS = GROUPS // SLOTS
    FIRST_B = BODIES_0 + QUADS + 2
    LAST = BODIES - 1
    LIGHT = PAIRS - 1 - (BODIES - FIRST_B)
    HEAVY = BODIES - FIRST_B - LIGHT
    assert LIGHT > 1 and HEAVY > 1
    ZERO_CHUNKS = BODIES_0 * SLOTS + EARLY_CLEARS
    ZERO_CHUNK = -(-N * D // (P * ZERO_CHUNKS))
    assert D == P and ZERO_CHUNK <= 4 * ROWS

    ctx = ExitStack()
    with ctx:
        def sb(name, shape, dt=FP32):
            return ctx.enter_context(nc.sbuf_tensor(name, shape, dt))

        def ps(name):
            return ctx.enter_context(nc.psum_tensor(name, [P, ROWS], FP32))

        def sem(name):
            return ctx.enter_context(nc.semaphore(name))

        def sems(name, n):
            return [sem(f"{name}{i}") for i in range(n)]

        out0_table = nc.dram_tensor("out0_table", [ZERO_CHUNK * ZERO_CHUNKS, D], FP32, kind="Internal").ap()
        x1eT_spill = nc.dram_tensor("x1eT_spill", [P, GROUPS * ROWS], FP32, kind="Internal").ap()
        mask_dram = nc.dram_tensor("mask_dram", [2, ETILES, P], BF16, kind="Internal").ap()

        ident = sb("ident", [P, P])
        center = sb("center", [P, P])
        raw = sb("raw", [P, 6, P])
        W1A, W1B, EW2, W1R, W2R, RES = range(6)
        wd = sb("wd", [P, P])
        wc1 = sb("wc1", [P, P])
        wc2 = sb("wc2", [P, P])
        wcr = sb("wcr", [P, P])
        wtmp = sb("wtmp", [P, 3, P])
        bias_cols = sb("bias_cols", [P, 3])
        brow = sb("brow", [P, 4, P])
        bpart = sb("bpart", [P, 3, P], BF16)
        bias_rhs = sb("bias_rhs", [P, TILES, P], BF16)
        ones_bf = sb("ones_bf", [P, P], BF16)
        bsum = sb("bsum", [P, 2])
        eps_col = sb("eps_col", [P, 1])

        shared = sb("shared", [P, 6, ROWS])
        index_rows = shared[:, :, :].rearrange("p n d -> p (n d)")[:, 0:20 * P]
        index_rows = index_rows.rearrange("p (a n h e) -> p a n h e", a=2, n=5, h=2)
        idx_in = index_rows[:, 0].bitcast(I32)
        idx_f = index_rows[:, 1]
        same = sb("same", [P, 2, P])
        mask_rows = sb("mask_rows", [P, 2, 2, P], BF16)
        idx = sb("idx", [P, 3, 2 * P], I32)

        WHOLE = E // ROWS
        last_dst = sb("last_dst", [1, WHOLE], I32)
        stores_16 = sb("stores_16", [1, WHOLE], I32)

        x_in = sb("x_in", [P, SLOTS, ROWS])
        x1 = sb("x1", [P, 2, ROWS])
        xT = sb("xT", [P, SLOTS, ROWS])
        hT = sb("hT", [P, 2, ROWS])
        o_rows = sb("o_rows", [P, SLOTS, ROWS])
        bn_a = sb("bn_a", [P, 2, TILES, 6])
        mv_a = sb("mv_a", [P, SLOTS, TILES, 2])
        sd_a = sb("sd_a", [P, SLOTS, TILES])
        rs_a = sb("rs_a", [P, SLOTS, TILES])
        bn_b = sb("bn_b", [P, 2, TILES, 6])
        mv_b = sb("mv_b", [P, SLOTS, TILES, 2])
        sd_b = sb("sd_b", [P, SLOTS, TILES])
        rs_b = sb("rs_b", [P, SLOTS, TILES])

        edge_rows = sb("edge_rows", [P, ETILES * P])
        xs_rows = sb("xs_rows", [P, 2, ROWS])
        xd_rows = sb("xd_rows", [P, SLOTS, ROWS])
        xsT = sb("xsT", [P, 2, ROWS])
        xdT = sb("xdT", [P, 2, ROWS])
        ehT = sb("ehT", [P, 2, ROWS])
        msgT = sb("msgT", [P, 2, ROWS])
        scanT, out0_rows, z_rows = shared[:, 0:2, :], shared[:, 2:4, :], shared[:, 4:6, :]
        shared_x1e = sb("shared_x1e", [P, 4, ROWS])
        x1e_rows, x1eT = shared_x1e[:, 0:2, :], shared_x1e[:, 2:4, :]
        zeros = shared_x1e[:, :, :].rearrange("p n d -> p (n d)")[:, 0:ZERO_CHUNK]
        mask = sb("mask", [P, 2, ROWS], BF16)
        bn_e = sb("bn_e", [P, 2, TILES, 6])
        mv_e = sb("mv_e", [P, 2, TILES, 2])
        sd_e = sb("sd_e", [P, 2, TILES])
        rs_e = sb("rs_e", [P, 2, TILES])
        squares = sb("squares", [P, 2, ROWS])
        sum_sq = sb("sum_sq", [P, 2, TILES])
        sd_y = sb("sd_y", [P, 2, TILES])
        rs_y = sb("rs_y", [P, 2, TILES])
        zsT_sum = scanT
        sumT = xsT
        eh2T = ehT

        psT = ps("psT")
        psH = ps("psH")
        psY = [ps("psY0"), ps("psY1")]
        psE = [ps(f"psE{i}") for i in range(4)]

        s_w = sem("weights_loaded")
        s_i = sem("indices_loaded")
        s_iz = sem("index_pads_written")
        s_last = sem("last_dst_loaded")
        s_c = sem("constants_built")
        s_turn = sem("scatter_turn")
        s_c2 = sem("center_built")
        s_dv = sem("setup_vector_steps")
        s_pe = sem("setup_tensor_steps")
        s_mst = sem("masks_stored")
        s_zt = sem("zero_tile_written")
        table_cleared = sem("table_cleared")
        x_loaded = sems("x_loaded", SLOTS)
        stored = sems("stored", SLOTS)
        bn1_done = sem("bn1_done")
        var1_done = sem("var1_done")
        std1_done = sem("std1_done")
        rstd1_done = sem("rstd1_done")
        x1_done = sem("x1_done")
        t_done = sem("t_done")
        xT_done = sem("xT_done")
        w1_done = sem("w1_done")
        hT_done = sem("hT_done")
        y_done = sem("y_done")
        bn2_done = sem("bn2_done")
        var2_done = sem("var2_done")
        std2_done = sem("std2_done")
        rstd2_done = sem("rstd2_done")
        o_done = sem("o_done")
        src_gathered = sems("src_gathered", SLOTS)
        xs_copied = sems("xs_copied", 2)
        dst_gathered = sems("dst_gathered", 2)
        mask_loaded = sems("mask_loaded", 2)
        tx_done = sem("tx_done")
        xsdT_done = sem("xsdT_done")
        eh_done = sem("eh_done")
        ehT_done = sem("ehT_done")
        m_done = sem("m_done")
        msg_done = sem("msg_done")
        max_done = sem("max_done")
        bt_done = sem("bt_done")
        out0_done = sem("out0_done")
        z_done = sem("z_done")
        bne_done = sem("bne_done")
        vare_done = sem("vare_done")
        stde_done = sem("stde_done")
        rstde_done = sem("rstde_done")
        x1e_done = sem("x1e_done")
        xt_done = sem("xt_done")
        x1eT_done = sem("x1eT_done")
        spilled = sems("spilled", 2)
        scattered = sems("scattered", 2)
        z_gathered = sems("z_gathered", 2)
        maskb_loaded = sems("maskb_loaded", 2)
        x1eT_loaded = sems("x1eT_loaded", 2)
        bnz_done = sem("bnz_done")
        varz_done = sem("varz_done")
        stdz_done = sem("stdz_done")
        rstdz_done = sem("rstdz_done")
        x1s_done = sem("x1s_done")
        zt_done = sem("zt_done")
        sum_done = sem("sum_done")
        hsum_done = sem("hsum_done")
        we_done = sem("we_done")
        eh2_done = sem("eh2_done")
        ye_done = sem("ye_done")
        sumsq_done = sem("sumsq_done")
        stdy_done = sem("stdy_done")
        rstdy_done = sem("rstdy_done")
        res_done = sem("res_done")
        final = sems("final", 2)

        WEIGHT_STEPS = 15
        IDX_STEP = WEIGHT_STEPS + 6
        SETUP_STEPS = 22
        BODY_SHIFT = (SLOTS * ROWS).bit_length() - 1
        assert SLOTS * ROWS == 1 << BODY_SHIFT

        def unit(b, k):
            return b + k // SLOTS, k % SLOTS

        def is_unit(b, k):
            return not isinstance(b, int) or 0 <= b * SLOTS + k < UNITS

        def is_quad(j, r):
            return not isinstance(j, int) or 0 <= j * SLOTS + r < GROUPS

        def group(i, q):
            return i + q // 2, q % 2

        def is_group(i, q):
            return not isinstance(i, int) or 0 <= 2 * i + q < GROUPS

        def wait(eng, s, n):
            if not isinstance(n, int) or n > 0:
                eng.wait_ge(s, n)

        def tiles(ap):
            return ap.rearrange("p (t d) -> p t d", t=TILES)

        def cut(t):
            return slice(t * P, (t + 1) * P)

        def walk(eng, dense, step_a, lead_b, step_b):
            def body(b):
                for k in range(SLOTS):
                    dense(b, k)

            def quad(j, b):
                for r in range(SLOTS):
                    step_a(j, r, b)

            def pair(i, b):
                for q in range(2):
                    step_b(i, q, b, 2 * q, 0 if b is None else 2)

            def two_pairs(i, b):
                for k in range(SLOTS):
                    step_b(i + k // 2, k % 2, b, k, 1)

            body(0)
            body(1)
            with eng.Fori(2, BODIES_0) as b:
                body(b)
            quad(0, BODIES_0)
            with eng.Fori(1, QUADS) as j:
                quad(j, j + BODIES_0)
            quad(QUADS, FIRST_B - 2)
            body(FIRST_B - 1)
            lead_b()
            pair(0, FIRST_B)
            with eng.Fori(1, HEAVY) as i:
                pair(i, i + FIRST_B)
            with eng.Fori(0, LIGHT - 1) as n:
                two_pairs(n * 2 + HEAVY, n + (FIRST_B + HEAVY))
            two_pairs(HEAVY + 2 * (LIGHT - 1), LAST)
            pair(PAIRS - 1, None)
            for k in range(3):
                dense(LAST + 1, k)
            pair(PAIRS, None)

        block = ctx.enter_context(nc.Block())

        @block.sync
        def _(sp):
            def number(n, top):
                return n if isinstance(n, int) else sp.snap(n, min_val=-1, max_val=top)

            def rows_of(a, b, k):
                base = (b * SLOTS + k) * ROWS
                base = min(base, N - ROWS) if isinstance(b, int) else number(base, N - ROWS)
                return a[bass.ds(base, ROWS), :].rearrange("(p r) d -> p (r d)", p=P)

            table = out0_table.rearrange("n d -> (n d)").rearrange("(p f) -> p f", p=P)

            def load(b, k):
                b, k = unit(b, k)
                if is_unit(b, k):
                    rows = rows_of(x, b, k)
                    wait(sp, x1_done, (b - 1) * SLOTS + k + 1)
                    sp.dma_start(x_in[:, k, :], rows).then_inc(x_loaded[k], 16)

            def store(b, k):
                b, k = unit(b, k)
                if is_unit(b, k):
                    rows = rows_of(out, b, k)
                    wait(sp, o_done, b * SLOTS + k + 1)
                    if isinstance(b, int) and b * SLOTS + k == UNITS - 1:
                        sp.wait_ge(stored[(k - 1) % SLOTS], 16 * (b + (k - 1) // SLOTS + 1))
                    sp.dma_start(rows, o_rows[:, k, :]).then_inc(stored[k], 16)

            def clear(b, k):
                at = number((b * SLOTS + k) * ZERO_CHUNK, (ZERO_CHUNKS - 1) * ZERO_CHUNK)
                sp.dma_start(table[:, bass.ds(at, ZERO_CHUNK)], zeros).then_inc(table_cleared, 16)

            def dense(b, k, clears=True):
                load(b, k + 3)
                store(b, k - 5)
                if clears and (not isinstance(b, int) or b < BODIES_0):
                    clear(b, k)
                if isinstance(b, int) and b * SLOTS + k == UNITS + 2:
                    store(b, -2)
                    store(b, -1)

            def feed_a(j, r):
                j, r = unit(j, r)
                if is_quad(j, r):
                    g, q = j * SLOTS + r, r % 2
                    at = number(g * ROWS, (GROUPS - 1) * ROWS)
                    wait(sp, tx_done, g - 1)
                    wait(sp, max_done, g - 1)
                    wait(sp, src_gathered[r], 16 * TILES * (j + 1))
                    sp.dma_start(xs_rows[:, q, :], edge_rows[:, bass.ds(at, ROWS)]).then_inc(xs_copied[q], 16)
                    sp.dma_start(mask[:, q, :], mask_dram[0].rearrange("t e -> (t e)")[bass.ds(at, ROWS)]
                                 .unsqueeze(0).broadcast_to([P, ROWS])).then_inc(mask_loaded[q], 16)

            def spill(j, r):
                j, r = unit(j, r)
                if is_quad(j, r):
                    g, q = j * SLOTS + r, r % 2
                    at = number(g * ROWS, (GROUPS - 1) * ROWS)
                    wait(sp, x1eT_done, g + 1)
                    sp.dma_start(x1eT_spill[:, bass.ds(at, ROWS)], x1eT[:, q, :]).then_inc(spilled[q], 16)

            def step_a(j, r, b):
                if isinstance(j, int) and j + r == 0:
                    sp.wait_ge(s_mst, 64)
                    feed_a(0, 0)
                if b is not None:
                    dense(b, r, clears=False)
                spill(j, r - 3)
                feed_a(j, r + 1)

            def feed_b(i, q):
                if is_group(i, q):
                    g = 2 * i + q
                    at = number(g * ROWS, (GROUPS - 1) * ROWS)
                    wait(sp, sum_done, g - 1)
                    wait(sp, ye_done, g - 1)
                    sp.dma_start(mask[:, q, :], mask_dram[1].rearrange("t e -> (t e)")[bass.ds(at, ROWS)]
                                 .unsqueeze(0).broadcast_to([P, ROWS])).then_inc(maskb_loaded[q], 16)
                    sp.dma_start(x1eT[:, q, :], x1eT_spill[:, bass.ds(at, ROWS)]).then_inc(x1eT_loaded[q], 16)

            def lead_b():
                spill(QUADS, GROUPS - QUADS * SLOTS - 1)
                for q in range(2):
                    sp.wait_ge(spilled[q], 16 * PAIRS)
                sp.wait_ge(max_done, GROUPS)

            def step_b(i, q, b, k, units):
                if b is not None:
                    dense(b, k, clears=False)
                feed_b(i, q)
                if units == 2:
                    dense(b, k + 1, clears=False)

            for k in range(3):
                load(0, k)
            sp.wait_ge(s_zt, 1)
            sp.wait_ge(s_iz, 1)
            HALF = P * P
            for n, a in enumerate((src, dst, dst)):
                clear(BODIES_0, n)
                sp.dma_start(idx_in[:, n, 0, :], a[0:HALF].rearrange("(j p) -> j p", p=P)).then_inc(s_i, 16)
                sp.dma_start(idx_in[0:FULL - P, n, 1, :],
                             a[HALF:FULL * P].rearrange("(j p) -> j p", p=P)).then_inc(s_i, 16)
                sp.dma_start(idx_in[FULL - P:FULL - P + 1, n, 1, 0:REST],
                             a[FULL * P:E].rearrange("(j p) -> j p", j=1)).then_inc(s_i, 16)
            sp.dma_start(idx_in[:, 3, 0, :], dst[1:HALF + 1].rearrange("(j p) -> j p", p=P)).then_inc(s_i, 16)
            sp.dma_start(idx_in[0:FULL - P, 3, 1, :],
                         dst[HALF + 1:FULL * P + 1].rearrange("(j p) -> j p", p=P)).then_inc(s_i, 16)
            sp.dma_start(idx_in[FULL - P:FULL - P + 1, 3, 1, 0:REST - 1],
                         dst[FULL * P + 1:E].rearrange("(j p) -> j p", j=1)).then_inc(s_i, 16)
            sp.dma_start(idx_in[0:1, 4, 0, 1:P], dst[0:P - 1].rearrange("(j p) -> j p", j=1)).then_inc(s_i, 16)
            sp.dma_start(idx_in[1:P, 4, 0, :], dst[P - 1:HALF - 1].rearrange("(j p) -> j p", p=P)).then_inc(s_i, 16)
            sp.dma_start(idx_in[0:FULL - P, 4, 1, :],
                         dst[HALF - 1:FULL * P - 1].rearrange("(j p) -> j p", p=P)).then_inc(s_i, 16)
            sp.dma_start(idx_in[FULL - P:FULL - P + 1, 4, 1, 0:REST],
                         dst[FULL * P - 1:E - 1].rearrange("(j p) -> j p", j=1)).then_inc(s_i, 16)

            sp.dma_start(last_dst[0:1, :], dst[0:WHOLE * ROWS].rearrange("(o g e) -> o g e", o=1, e=ROWS)[:, :, ROWS - 1],
                         allow_slow_non_contiguous=True).then_inc(s_last, 16)
            for n in range(3, EARLY_CLEARS):
                clear(BODIES_0, n)
            sp.wait_ge(s_dv, WEIGHT_STEPS + 5)
            for m in range(2):
                for h in range(2):
                    n = P if h == 0 else ETILES - P
                    sp.dma_start(mask_dram[m, h * P:h * P + n, :], mask_rows[0:n, m, h, :]).then_inc(s_mst, 16)
            walk(sp, dense, step_a, lead_b, step_b)
            for k in range(SLOTS):
                sp.wait_ge(stored[k], 16 * BODIES)

        @block.gpsimd
        def _(pool):
            nc.gpsimd.memset(idx_in[:, 0:2, :, :], 0)
            nc.gpsimd.memset(idx_in[:, 2, :, :], BIG)
            nc.gpsimd.memset(idx_in[:, 3:5, :, :], -1).then_inc(s_iz, 1)
            nc.gpsimd.memset(ident[:, :], 0.0)
            nc.gpsimd.memset(center[:, :], -1.0 / P).then_inc(s_c2, 1)
            pool.wait_ge(s_c2, 1)
            nc.gpsimd.affine_select(out=ident[:, :], in_=ident[:, :], compare_op=ALU.not_equal, fill=1.0,
                                    base=0, pattern=[[-1, P]], channel_multiplier=1)
            nc.gpsimd.affine_select(out=center[:, :], in_=center[:, :], compare_op=ALU.not_equal, fill=1.0 - 1.0 / P,
                                    base=0, pattern=[[-1, P]], channel_multiplier=1).then_inc(s_c, 1)
            pool.wait_ge(s_dv, IDX_STEP)
            SRC, DST, SCAT = range(3)

            def gather(to, table, what, t, done, add=False):
                kw = dict(compute_op=ALU.add) if add else {}
                nc.gpsimd.indirect_dma_start(to, None, table, bass.IndirectOffsetOnAxis(idx[:, what, t:t + 1], 0),
                                             bounds_check=N - 1, oob_is_err=True, **kw).then_inc(done, 16)

            def scatter(table, frm, t, done):
                nc.gpsimd.indirect_dma_start(table, bass.IndirectOffsetOnAxis(idx[:, SCAT, t:t + 1], 0), frm, None,
                                             bounds_check=N - 1, oob_is_err=False).then_inc(done, 16)

            for g in range(GROUPS):
                j, r = divmod(g, SLOTS)
                wait(pool, src_gathered[r], 16 * TILES * j)
                for t in range(TILES):
                    gather(edge_rows[:, cut(g * TILES + t)], x, SRC, g * TILES + t, src_gathered[r])

            def gather_dst(g):
                i, q = divmod(g, 2)
                wait(pool, dst_gathered[q], 16 * TILES * i)
                wait(pool, z_done, g - 3)
                for t in range(TILES):
                    gather(xd_rows[:, g % SLOTS, cut(t)], x, DST, g * TILES + t, dst_gathered[q])

            for g in range(SLOTS):
                gather_dst(g)
            pool.wait_ge(table_cleared, 16 * ZERO_CHUNKS)
            for g in range(GROUPS):
                i, q = divmod(g, 2)
                pool.wait_ge(out0_done, g + 1)
                wait(pool, scattered[q], 16 * TILES * i)
                for t in range(TILES):
                    scatter(out0_table, out0_rows[:, q, cut(t)], g * TILES + t, scattered[q])
                if g + SLOTS < GROUPS:
                    gather_dst(g + SLOTS)

            for q in range(2):
                pool.wait_ge(scattered[q], 16 * TILES * PAIRS)
                pool.wait_ge(xs_copied[q], 16 * PAIRS)
            for g in range(GROUPS):
                i, q = divmod(g, 2)
                wait(pool, z_gathered[q], 16 * TILES * i)
                for t in range(TILES):
                    gather(edge_rows[:, cut(g * TILES + t)], out0_table, SRC, g * TILES + t, z_gathered[q], add=True)

            pool.wait_ge(s_dv, SETUP_STEPS)
            for g in range(GROUPS):
                i, q = divmod(g, 2)
                wait(pool, final[q], 16 * TILES * i)
                pool.wait_ge(res_done, g + 1)
                if g < WHOLE:
                    before = pool.value_load(stores_16[0:1, g:g + 1], min_val=0, max_val=16 * LAST)
                    count = pool.snap(before + 16)
                    for k in range(SLOTS):
                        pool.wait_ge(stored[k], count)
                    pool.nop().then_inc(s_turn, 1)
                elif g == WHOLE:
                    for k in range(SLOTS):
                        pool.wait_ge(stored[k], 16 * BODIES)
                for t in range(TILES):
                    scatter(out, edge_rows[:, cut(g * TILES + t)], g * TILES + t, final[q])
            for q in range(2):
                pool.wait_ge(final[q], 16 * TILES * PAIRS)

        @block.vector
        def _(dve):
            v = nc.vector
            step = [0]

            def link(ins):
                step[0] += 1
                ins.then_inc(s_dv, 1)
                dve.wait_ge(s_dv, step[0])

            def stats(bn, rows, done):
                for t in range(TILES):
                    last = v.bn_stats(bn[:, t, :], rows[:, cut(t)])
                last.then_inc(done, 1)

            def aggregate(mv, bn, done):
                for t in range(TILES):
                    last = v.bn_aggr(mv[:, t, :], bn[:, t, :])
                last.then_inc(done, 1)

            def scale(to, rows, rs, done):
                v.tensor_tensor(tiles(to), tiles(rows), rs.unsqueeze(2).broadcast_to([P, TILES, P]),
                                ALU.mult).then_inc(done, 1)

            def norm1_stats(b, k, which=range(TILES)):
                b, k = unit(b, k)
                if is_unit(b, k):
                    if which[0] == 0:
                        dve.wait_ge(x_loaded[k], 16 * (b + 1))
                    for t in which:
                        last = v.bn_stats(bn_a[:, k % 2, t, :], x_in[:, k, cut(t)])
                    if which[-1] == TILES - 1:
                        last.then_inc(bn1_done, 1)

            def norm1_ready(b, k):
                b, k = unit(b, k)
                if is_unit(b, k):
                    dve.wait_ge(bn1_done, b * SLOTS + k + 1)

            def norm1_var(b, k):
                b, k = unit(b, k)
                if is_unit(b, k):
                    aggregate(mv_a[:, k, :, :], bn_a[:, k % 2, :, :], var1_done)

            def norm1_recip(b, k):
                b, k = unit(b, k)
                if is_unit(b, k):
                    dve.wait_ge(std1_done, b * SLOTS + k + 1)
                    v.reciprocal(rs_a[:, k, :], sd_a[:, k, :]).then_inc(rstd1_done, 1)

            def norm1_scale(b, k):
                b, k = unit(b, k)
                if is_unit(b, k):
                    n = b * SLOTS + k
                    dve.wait_ge(rstd1_done, n + 1)
                    wait(dve, t_done, n - 1)
                    scale(x1[:, k % 2, :], x_in[:, k, :], rs_a[:, k, :], x1_done)

            def norm2_stats(b, k):
                b, k = unit(b, k)
                if is_unit(b, k):
                    dve.wait_ge(y_done, b * SLOTS + k + 1)
                    stats(bn_b[:, k % 2, :, :], psY[k % 2], bn2_done)

            def norm2_ready(b, k):
                b, k = unit(b, k)
                if is_unit(b, k):
                    dve.wait_ge(bn2_done, b * SLOTS + k + 1)

            def norm2_var(b, k):
                b, k = unit(b, k)
                if is_unit(b, k):
                    aggregate(mv_b[:, k, :, :], bn_b[:, k % 2, :, :], var2_done)

            def norm2_recip(b, k):
                b, k = unit(b, k)
                if is_unit(b, k):
                    dve.wait_ge(std2_done, b * SLOTS + k + 1)
                    v.reciprocal(rs_b[:, k, :], sd_b[:, k, :]).then_inc(rstd2_done, 1)

            def dense(b, k):
                norm1_ready(b, k + 2)
                norm2_stats(b, k - 3)
                norm1_var(b, k + 2)
                norm2_ready(b, k - 3)
                norm1_scale(b, k + 1)
                norm2_var(b, k - 3)
                norm1_recip(b, k + 2)
                norm1_stats(b, k + 3, range(0, 2))
                norm2_recip(b, k - 3)
                norm1_stats(b, k + 3, range(2, TILES))

            def residual0(j, r):
                j, r = unit(j, r)
                if is_quad(j, r):
                    g, q = j * SLOTS + r, r % 2
                    dve.wait_ge(out0_done, g + 1)
                    wait(dve, x1e_done, g - 1)
                    v.tensor_tensor(z_rows[:, q, :], out0_rows[:, q, :], xd_rows[:, r, :], ALU.add).then_inc(z_done, 1)
                    dve.wait_ge(z_done, g + 1)
                    stats(bn_e[:, q, :, :], z_rows[:, q, :], bne_done)

            def residual0_ready(j, r):
                j, r = unit(j, r)
                if is_quad(j, r):
                    dve.wait_ge(bne_done, j * SLOTS + r + 1)

            def residual0_var(j, r):
                j, r = unit(j, r)
                if is_quad(j, r):
                    aggregate(mv_e[:, r % 2, :, :], bn_e[:, r % 2, :, :], vare_done)

            def scale0(j, r):
                j, r = unit(j, r)
                if is_quad(j, r):
                    g, q = j * SLOTS + r, r % 2
                    dve.wait_ge(stde_done, g + 1)
                    v.reciprocal(rs_e[:, q, :], sd_e[:, q, :]).then_inc(rstde_done, 1)
                    dve.wait_ge(rstde_done, g + 1)
                    wait(dve, xt_done, g - 1)
                    if isinstance(j, int) and g == 0:
                        dve.wait_ge(table_cleared, 16 * ZERO_CHUNKS)
                    scale(x1e_rows[:, q, :], z_rows[:, q, :], rs_e[:, q, :], x1e_done)

            def segment_max(j, r):
                j, r = unit(j, r)
                if is_quad(j, r):
                    g, q = j * SLOTS + r, r % 2
                    first = isinstance(j, int) and g == 0
                    dve.wait_ge(mask_loaded[q], 16 * (2 * j + r // 2 + 1))
                    dve.wait_ge(msg_done, g + 1)
                    wait(dve, bt_done, g - 1)
                    wait(dve, max_done, g)
                    v.tensor_tensor_scan(scanT[:, q, :], mask[:, q, :], msgT[:, q, :],
                                         0.0 if first else scanT[:, 1 - q, ROWS - 1:ROWS],
                                         ALU.add, ALU.max).then_inc(max_done, 1)

            def step_a(j, r, b):
                k = r
                residual0_ready(j, r - 2)
                if b is not None:
                    norm1_ready(b, k + 2)
                    norm2_stats(b, k - 3)
                residual0_var(j, r - 2)
                if b is not None:
                    norm1_var(b, k + 2)
                scale0(j, r - 2)
                if b is not None:
                    norm2_ready(b, k - 3)
                    norm1_scale(b, k + 1)
                    norm2_var(b, k - 3)
                    norm1_recip(b, k + 2)
                    norm2_recip(b, k - 3)
                segment_max(j, r - 1)
                if b is not None:
                    norm1_stats(b, k + 3, range(TILES))
                residual0(j, r - 1)

            def src_stats(i, q):
                i, q = group(i, q)
                if is_group(i, q):
                    dve.wait_ge(z_gathered[q], 16 * TILES * (i + 1))
                    g = 2 * i + q
                    for t in range(TILES):
                        last = v.bn_stats(bn_e[:, q, t, :], edge_rows[:, bass.ds(g * ROWS + t * P, P)])
                    last.then_inc(bnz_done, 1)

            def src_ready(i, q):
                i, q = group(i, q)
                if is_group(i, q):
                    dve.wait_ge(bnz_done, 2 * i + q + 1)

            def src_var(i, q):
                i, q = group(i, q)
                if is_group(i, q):
                    aggregate(mv_e[:, q, :, :], bn_e[:, q, :, :], varz_done)

            def src_recip(i, q):
                i, q = group(i, q)
                if is_group(i, q):
                    dve.wait_ge(stdz_done, 2 * i + q + 1)
                    v.reciprocal(rs_e[:, q, :], sd_e[:, q, :]).then_inc(rstdz_done, 1)

            def src_scale(i, q):
                i, q = group(i, q)
                if is_group(i, q):
                    g = 2 * i + q
                    dve.wait_ge(rstdz_done, g + 1)
                    wait(dve, zt_done, g - 1)
                    scale(x1e_rows[:, q, :], edge_rows[:, bass.ds(g * ROWS, ROWS)], rs_e[:, q, :], x1s_done)

            def segment_sum(i, q):
                if is_group(i, q):
                    g = 2 * i + q
                    first = isinstance(i, int) and g == 0
                    dve.wait_ge(maskb_loaded[q], 16 * (i + 1))
                    dve.wait_ge(zt_done, g + 1)
                    wait(dve, sum_done, g)
                    v.tensor_tensor_scan(zsT_sum[:, q, :], mask[:, q, :], psE[0][:, :],
                                         0.0 if first else zsT_sum[:, 1 - q, ROWS - 1:ROWS],
                                         ALU.mult, ALU.add).then_inc(sum_done, 1)

            def add_dst(i, q):
                if is_group(i, q):
                    g = 2 * i + q
                    dve.wait_ge(x1eT_loaded[q], 16 * (i + 1))
                    dve.wait_ge(sum_done, g + 1)
                    wait(dve, we_done, g - 1)
                    v.tensor_tensor(sumT[:, q, :], zsT_sum[:, q, :], x1eT[:, q, :], ALU.add).then_inc(hsum_done, 1)

            def out_recip(i, q):
                i, q = group(i, q)
                if is_group(i, q):
                    dve.wait_ge(stdy_done, 2 * i + q + 1)
                    v.reciprocal(rs_y[:, q, :], sd_y[:, q, :]).then_inc(rstdy_done, 1)

            def lead_b():
                for q in range(2):
                    src_stats(0, q)
                    src_ready(0, q)
                    src_var(0, q)
                src_recip(0, 0)
                src_recip(0, 1)
                dve.wait_ge(xt_done, GROUPS)
                src_scale(0, 0)
                src_stats(0, 2)

            def step_b(i, q, b, k, units):
                src_ready(i, q + 2)
                if b is not None:
                    norm1_ready(b, k + 2)
                    norm2_stats(b, k - 3)
                    src_var(i, q + 2)
                    norm1_var(b, k + 2)
                    norm2_ready(b, k - 3)
                    norm1_scale(b, k + 1)
                    norm2_var(b, k - 3)
                src_scale(i, q + 1)
                if b is None:
                    src_var(i, q + 2)
                src_recip(i, q + 2)
                segment_sum(i, q)
                if b is not None:
                    norm1_recip(b, k + 2)
                    norm2_recip(b, k - 3)
                add_dst(i, q)
                out_recip(i, q - 2)
                if b is not None:
                    norm1_stats(b, k + 3)
                src_stats(i, q + 3)
                if units == 2:
                    dense(b, k + 1)

            v.memset(zeros, 0.0).then_inc(s_zt, 1)
            v.memset(eps_col[:, :], EPS)
            v.memset(ones_bf[:, :], 1.0)
            norm1_stats(0, 0)
            norm1_ready(0, 0)
            norm1_var(0, 0)
            norm1_stats(0, 1)
            norm1_ready(0, 1)
            norm1_recip(0, 0)
            norm1_var(0, 1)
            norm1_scale(0, 0)
            norm1_recip(0, 1)
            norm1_stats(0, 2)

            dve.wait_ge(s_w, 16 * 11)
            dve.wait_ge(s_c, 1)
            v.tensor_tensor(wd[:, :], raw[:, W1A, :], raw[:, W1B, :], ALU.subtract)
            link(v.tensor_tensor(wtmp[:, 0, :], raw[:, RES, :], ident[:, :], ALU.add))
            dve.wait_ge(s_pe, 1)
            v.tensor_copy(wc1[:, :], psE[2][:, 0:P])
            link(v.tensor_copy(wtmp[:, 1:3, :], psE[2][:, P:3 * P].rearrange("p (a b) -> p a b", a=2)))
            link(v.tensor_tensor(brow[:, 2, :], brow[:, 0, :], brow[:, 1, :], ALU.add))
            link(v.reduce_sum(bsum[:, 0:1], brow[:, 2, :], axis=AX.X))
            link(v.tensor_scalar(bsum[:, 1:2], bsum[:, 0:1], 1.0 / P, None, ALU.mult))
            link(v.tensor_scalar(brow[:, 2, :], brow[:, 2, :], bsum[:, 1:2], None, ALU.subtract))
            link(v.tensor_copy(bpart[:, 0, :], brow[:, 2, :]))
            link(v.tensor_tensor(brow[:, 3, :], brow[:, 2, :], bpart[:, 0, :], ALU.subtract))
            link(v.tensor_copy(bpart[:, 1, :], brow[:, 3, :]))
            link(v.tensor_tensor(brow[:, 2, :], brow[:, 3, :], bpart[:, 1, :], ALU.subtract))
            link(v.tensor_copy(bpart[:, 2, :], brow[:, 2, :]))
            link(v.tensor_scalar(brow[:, 0, :], bpart[:, 0, :], ident[:, 0:1], None, ALU.mult))
            dve.wait_ge(s_pe, 2)
            v.tensor_copy(wcr[:, :], psE[3][:, 0:P])
            v.tensor_copy(wc2[:, :], psE[3][:, P:2 * P])
            for n in (1, 2):
                link(v.scalar_tensor_tensor(out=brow[:, n % 2, :], in0=bpart[:, n, :], scalar=ident[:, n:n + 1],
                                            in1=brow[:, (n + 1) % 2, :], op0=ALU.mult, op1=ALU.add))
            for t in range(TILES):
                last = v.tensor_copy(bias_rhs[:, t, :], brow[:, 0, :])
            link(last)
            assert step[0] == WEIGHT_STEPS
            dve.wait_ge(s_i, 16 * 16)
            link(v.tensor_copy(idx_f[:, :, :, :], idx_in[:, :, :, :]))
            link(v.tensor_tensor(same[:, :, :], idx_f[:, 1, :, :], idx_f[:, 3, :, :], ALU.is_equal))
            link(v.scalar_tensor_tensor(out=idx_f[:, 2, :, :], in0=same[:, :, :], scalar=float(BIG),
                                        in1=idx_f[:, 2, :, :], op0=ALU.mult, op1=ALU.add))
            link(v.tensor_tensor(same[:, :, :], idx_f[:, 1, :, :], idx_f[:, 4, :, :], ALU.is_equal))
            v.tensor_scalar(mask_rows[:, 0, :, :], same[:, :, :], 1.0, -LOWEST, ALU.subtract, ALU.mult)
            link(v.tensor_copy(mask_rows[:, 1, :, :], same[:, :, :]))
            dve.wait_ge(s_pe, 3)
            v.tensor_copy(idx[:, 0, :], psE[0][:, 0:2 * P])
            v.tensor_copy(idx[:, 1, :], psE[0][:, 2 * P:4 * P])
            link(v.tensor_copy(idx[:, 2, :], psE[1][:, 0:2 * P]))
            assert step[0] == IDX_STEP
            dve.wait_ge(s_last, 16)
            link(v.tensor_scalar(stores_16[:, :], last_dst[:, :], BODY_SHIFT, 4, ALU.arith_shift_right,
                                 ALU.logical_shift_left))
            assert step[0] == SETUP_STEPS
            walk(dve, dense, step_a, lead_b, step_b)

        @block.scalar
        def _(act):
            a = nc.scalar
            for n, w in enumerate((e_w1[0:P, :], e_w1[P:2 * P, :], e_w2, w1, w2, wres)):
                act.dma_start(raw[:, n, :], w).then_inc(s_w, 16)
            for n, c in enumerate((e_b1, e_b2, b1)):
                act.dma_start(bias_cols[:, n:n + 1], c.rearrange("(p o) -> p o", o=1)).then_inc(s_w, 16)
            for n, r in enumerate((b2, bres)):
                act.dma_start(brow[:, n, :], r.unsqueeze(0).broadcast_to([P, P])).then_inc(s_w, 16)

            def relu(b, k):
                b, k = unit(b, k)
                if is_unit(b, k):
                    n = b * SLOTS + k
                    act.wait_ge(w1_done, n + 1)
                    wait(act, y_done, n - 1)
                    a.activation(hT[:, k % 2, :], psH[:, :], ACT.Relu, bias=bias_cols[:, 2:3]).then_inc(hT_done, 1)

            def copy_xT(b, k):
                b, k = unit(b, k)
                if is_unit(b, k):
                    n = b * SLOTS + k
                    act.wait_ge(t_done, n + 1)
                    wait(act, y_done, n - 3)
                    a.copy(xT[:, k, :], psT[:, :]).then_inc(xT_done, 1)

            def root(sd, mv, done):
                a.activation(sd, mv[:, :, 1], ACT.Sqrt, bias=eps_col[:, 0:1]).then_inc(done, 1)

            def root1(b, k):
                b, k = unit(b, k)
                if is_unit(b, k):
                    act.wait_ge(var1_done, b * SLOTS + k + 1)
                    root(sd_a[:, k, :], mv_a[:, k, :, :], std1_done)

            def root2(b, k):
                b, k = unit(b, k)
                if is_unit(b, k):
                    act.wait_ge(var2_done, b * SLOTS + k + 1)
                    root(sd_b[:, k, :], mv_b[:, k, :, :], std2_done)

            def finish(b, k):
                b, k = unit(b, k)
                if is_unit(b, k):
                    act.wait_ge(rstd2_done, b * SLOTS + k + 1)
                    wait(act, stored[k], 16 * b)
                    for t in range(TILES):
                        last = a.activation(o_rows[:, k, cut(t)], psY[k % 2][:, cut(t)], ACT.Copy,
                                            scale=rs_b[:, k, t:t + 1])
                    last.then_inc(o_done, 1)

            def first_half(b, k):
                root1(b, k + 2)
                relu(b, k - 1)
                copy_xT(b, k)

            def second_half(b, k):
                root2(b, k - 3)
                finish(b, k - 3)

            def dense(b, k):
                first_half(b, k)
                second_half(b, k)

            def copy_xsd(j, r):
                if is_quad(j, r):
                    g, q = j * SLOTS + r, r % 2
                    act.wait_ge(tx_done, g + 1)
                    wait(act, eh_done, g - 1)
                    a.copy(xsT[:, q, :], psE[0][:, :])
                    a.copy(xdT[:, q, :], psE[1][:, :]).then_inc(xsdT_done, 1)

            def relu0(j, r):
                j, r = unit(j, r)
                if is_quad(j, r):
                    g, q = j * SLOTS + r, r % 2
                    act.wait_ge(eh_done, g + 1)
                    wait(act, m_done, g - 1)
                    a.activation(ehT[:, q, :], psE[2][:, :], ACT.Relu, bias=bias_cols[:, 0:1]).then_inc(ehT_done, 1)

            def message(j, r):
                j, r = unit(j, r)
                if is_quad(j, r):
                    g, q = j * SLOTS + r, r % 2
                    act.wait_ge(m_done, g + 1)
                    wait(act, max_done, g - 1)
                    a.activation(msgT[:, q, :], psE[3][:, :], ACT.Identity, bias=bias_cols[:, 1:2]).then_inc(msg_done, 1)

            def copy_out0(j, r):
                j, r = unit(j, r)
                if is_quad(j, r):
                    g, q = j * SLOTS + r, r % 2
                    act.wait_ge(bt_done, g + 1)
                    wait(act, scattered[q], 16 * TILES * (2 * j + r // 2))
                    wait(act, z_done, g - 1)
                    a.copy(out0_rows[:, q, :], psE[3][:, :]).then_inc(out0_done, 1)

            def root0(j, r):
                j, r = unit(j, r)
                if is_quad(j, r):
                    act.wait_ge(vare_done, j * SLOTS + r + 1)
                    root(sd_e[:, r % 2, :], mv_e[:, r % 2, :, :], stde_done)

            def copy_x1eT(j, r):
                j, r = unit(j, r)
                if is_quad(j, r):
                    g, q = j * SLOTS + r, r % 2
                    act.wait_ge(xt_done, g + 1)
                    wait(act, spilled[q], 16 * (2 * j + r // 2))
                    a.copy(x1eT[:, q, :], psE[2][:, :]).then_inc(x1eT_done, 1)

            def step_a(j, r, b):
                relu0(j, r - 1)
                if b is not None:
                    relu(b, r - 1)
                root0(j, r - 2)
                if b is not None:
                    root1(b, r + 2)
                    copy_xT(b, r)
                message(j, r - 1)
                if b is not None:
                    root2(b, r - 3)
                copy_xsd(j, r)
                copy_x1eT(j, r - 2)
                if b is not None:
                    finish(b, r - 3)
                copy_out0(j, r - 1)

            def root_src(i, q):
                i, q = group(i, q)
                if is_group(i, q):
                    act.wait_ge(varz_done, 2 * i + q + 1)
                    root(sd_e[:, q, :], mv_e[:, q, :, :], stdz_done)

            def relu1(i, q):
                i, q = group(i, q)
                if is_group(i, q):
                    g = 2 * i + q
                    act.wait_ge(we_done, g + 1)
                    wait(act, ye_done, g - 1)
                    a.activation(eh2T[:, q, :], psE[1][:, :], ACT.Relu, bias=bias_cols[:, 2:3]).then_inc(eh2_done, 1)

            def square_sums(i, q):
                i, q = group(i, q)
                if is_group(i, q):
                    g = 2 * i + q
                    act.wait_ge(ye_done, g + 1)
                    for t in range(TILES):
                        last = a.activation(squares[:, q, cut(t)], psE[2 + q][:, cut(t)], ACT.Square,
                                            accum_out=sum_sq[:, q, t:t + 1])
                    last.then_inc(sumsq_done, 1)

            def root_out(i, q):
                i, q = group(i, q)
                if is_group(i, q):
                    act.wait_ge(sumsq_done, 2 * i + q + 1)
                    a.activation(sd_y[:, q, :], sum_sq[:, q, :], ACT.Sqrt, bias=eps_col[:, 0:1],
                                 scale=1.0 / P).then_inc(stdy_done, 1)

            def finish1(i, q):
                i, q = group(i, q)
                if is_group(i, q):
                    g = 2 * i + q
                    act.wait_ge(rstdy_done, g + 1)
                    for t in range(TILES):
                        last = a.activation(edge_rows[:, bass.ds(g * ROWS + t * P, P)], psE[2 + q][:, cut(t)],
                                            ACT.Copy, scale=rs_y[:, q, t:t + 1])
                    last.then_inc(res_done, 1)

            def lead_b():
                root_src(0, 0)
                root_src(0, 1)

            def step_b(i, q, b, k, units):
                root_src(i, q + 2)
                if b is not None:
                    first_half(b, k)
                relu1(i, q - 1)
                if b is not None:
                    root2(b, k - 3)
                square_sums(i, q - 2)
                root_out(i, q - 2)
                if b is not None:
                    finish(b, k - 3)
                finish1(i, q - 2)
                if units == 2:
                    dense(b, k + 1)

            root1(0, 0)
            root1(0, 1)
            act.wait_ge(s_w, 16 * 11)
            walk(act, dense, step_a, lead_b, step_b)

        @block.tensor
        def _(pe):
            t_ = nc.tensor
            pe.wait_ge(s_c, 1)
            pe.wait_ge(s_w, 16 * 11)
            pe.wait_ge(s_dv, 1)
            t_.matmul(psE[2][:, 0:P], center[:, :], raw[:, W1R, :], start=True, stop=True)
            t_.matmul(psE[2][:, P:2 * P], wtmp[:, 0, :], center[:, :], start=True, stop=True)
            t_.transpose(psE[2][:, 2 * P:3 * P], raw[:, W2R, :], ident[:, :]).then_inc(s_pe, 1)
            pe.wait_ge(s_dv, 2)
            t_.matmul(psE[3][:, 0:P], wtmp[:, 1, :], center[:, :], start=True, stop=True)
            t_.matmul(psE[3][:, P:2 * P], wtmp[:, 2, :], center[:, :], start=True, stop=True).then_inc(s_pe, 1)
            pe.wait_ge(s_dv, WEIGHT_STEPS + 3)
            for n in range(3):
                for h in range(2):
                    at = 2 * n + h
                    last = t_.transpose(psE[at // 4][:, cut(at % 4)], idx_f[:, n, h, :], ident[:, :])
            last.then_inc(s_pe, 1)
            pe.wait_ge(s_dv, IDX_STEP)

            def transpose4(to, rows, done=None):
                for t in range(TILES):
                    last = t_.transpose(to[:, cut(t)], rows[:, cut(t)], ident[:, :])
                if done is not None:
                    last.then_inc(done, 1)

            def product_rows(to, h, xt, done):
                t_.matmul(to[:, :], ones_bf[:, :], bias_rhs[:, :, :].rearrange("p t d -> p (t d)"),
                          start=True, stop=False, skip_group_check=True)
                for t in range(TILES):
                    t_.matmul(to[:, cut(t)], h[:, cut(t)], wc2[:, :], start=False, stop=False, skip_group_check=True)
                    last = t_.matmul(to[:, cut(t)], xt[:, cut(t)], wcr[:, :], start=False, stop=t == TILES - 1,
                                     skip_group_check=True)
                last.then_inc(done, 1)

            def first_product(b, k):
                b, k = unit(b, k)
                if is_unit(b, k):
                    n = b * SLOTS + k
                    pe.wait_ge(xT_done, n + 1)
                    wait(pe, hT_done, n)
                    t_.matmul(psH[:, :], wc1[:, :], xT[:, k, :], start=True, stop=True).then_inc(w1_done, 1)

            def transposed(b, k):
                b, k = unit(b, k)
                if is_unit(b, k):
                    n = b * SLOTS + k
                    pe.wait_ge(x1_done, n + 1)
                    wait(pe, xT_done, n)
                    transpose4(psT, x1[:, k % 2, :], t_done)

            def second_product(b, k):
                b, k = unit(b, k)
                if is_unit(b, k):
                    n = b * SLOTS + k
                    pe.wait_ge(hT_done, n + 1)
                    wait(pe, o_done, n - 1)
                    product_rows(psY[k % 2], hT[:, k % 2, :], xT[:, k, :], y_done)

            def first_half(b, k):
                first_product(b, k - 1)
                transposed(b, k)

            def dense(b, k):
                first_half(b, k)
                second_product(b, k - 2)

            def transpose_in(j, r):
                if is_quad(j, r):
                    g, q = j * SLOTS + r, r % 2
                    pe.wait_ge(xs_copied[q], 16 * (2 * j + r // 2 + 1))
                    pe.wait_ge(dst_gathered[q], 16 * TILES * (2 * j + r // 2 + 1))
                    wait(pe, xsdT_done, g)
                    transpose4(psE[0], xs_rows[:, q, :])
                    transpose4(psE[1], xd_rows[:, r, :], tx_done)

            def edge_product1(j, r):
                if is_quad(j, r):
                    g, q = j * SLOTS + r, r % 2
                    pe.wait_ge(xsdT_done, g + 1)
                    wait(pe, ehT_done, g)
                    wait(pe, x1eT_done, g - 1)
                    t_.matmul(psE[2][:, :], wd[:, :], xdT[:, q, :], start=True, stop=False)
                    t_.matmul(psE[2][:, :], raw[:, W1B, :], xsT[:, q, :], start=False, stop=True).then_inc(eh_done, 1)

            def edge_product2(j, r):
                j, r = unit(j, r)
                if is_quad(j, r):
                    g, q = j * SLOTS + r, r % 2
                    pe.wait_ge(ehT_done, g + 1)
                    wait(pe, out0_done, g)
                    t_.matmul(psE[3][:, :], raw[:, EW2, :], ehT[:, q, :], start=True, stop=True).then_inc(m_done, 1)

            def transpose_max(j, r):
                j, r = unit(j, r)
                if is_quad(j, r):
                    g, q = j * SLOTS + r, r % 2
                    pe.wait_ge(max_done, g + 1)
                    transpose4(psE[3], scanT[:, q, :], bt_done)

            def transpose_x1e(j, r):
                j, r = unit(j, r)
                if is_quad(j, r):
                    g, q = j * SLOTS + r, r % 2
                    pe.wait_ge(x1e_done, g + 1)
                    wait(pe, ehT_done, min(g + 2, GROUPS) if isinstance(g, int) else g + 2)
                    transpose4(psE[2], x1e_rows[:, q, :], xt_done)

            def step_a(j, r, b):
                if b is not None:
                    first_half(b, r)
                edge_product2(j, r - 1)
                transpose_in(j, r)
                transpose_x1e(j, r - 2)
                if b is not None:
                    second_product(b, r - 2)
                transpose_max(j, r - 1)
                edge_product1(j, r)

            def transpose_src(i, q):
                if is_group(i, q):
                    g = 2 * i + q
                    pe.wait_ge(x1s_done, g + 1)
                    wait(pe, sum_done, g)
                    transpose4(psE[0], x1e_rows[:, q, :], zt_done)

            def edge_product3(i, q):
                i, q = group(i, q)
                if is_group(i, q):
                    g = 2 * i + q
                    pe.wait_ge(hsum_done, g + 1)
                    wait(pe, eh2_done, g)
                    t_.matmul(psE[1][:, :], wc1[:, :], sumT[:, q, :], start=True, stop=True).then_inc(we_done, 1)

            def edge_product4(i, q):
                i, q = group(i, q)
                if is_group(i, q):
                    g = 2 * i + q
                    pe.wait_ge(eh2_done, g + 1)
                    wait(pe, res_done, g - 1)
                    product_rows(psE[2 + q], eh2T[:, q, :], x1eT[:, q, :], ye_done)

            def step_b(i, q, b, k, units):
                if b is not None:
                    first_half(b, k)
                edge_product3(i, q - 1)
                transpose_src(i, q)
                if b is not None:
                    second_product(b, k - 2)
                edge_product4(i, q - 1)
                if units == 2:
                    dense(b, k + 1)

            def lead_b():
                pe.wait_ge(xsdT_done, GROUPS)
                pe.wait_ge(x1eT_done, GROUPS)
                pe.wait_ge(out0_done, GROUPS)

            walk(pe, dense, step_a, lead_b, step_b)


_INS = ["x", "src", "dst", "L0_gnn_W1", "L0_gnn_b1", "L0_gnn_W2", "L0_gnn_b2", "L1_gnn_W1", "L1_gnn_b1",
        "L1_gnn_W2", "L1_gnn_b2", "L1_gnn_Wres", "L1_gnn_bres"]


def kernel(**inputs):
    import numpy as np
    import concourse.bacc as bacc
    from concourse.bass_utils import run_bass_kernel_spmd

    nc = bacc.Bacc("TRN2", target_bir_lowering=False, num_devices=1)
    arrays, args = {}, []
    for name in _INS:
        a = np.ascontiguousarray(inputs[name])
        arrays[f"in_{name}"] = a
        args.append(nc.dram_tensor(f"in_{name}", a.shape, mybir.dt.from_np(a.dtype), kind="ExternalInput").ap())
    shape = inputs["x"].shape
    args.append(nc.dram_tensor("out_0", shape, FP32, kind="ExternalOutput").ap())
    gnn_program(nc, *args)
    r = run_bass_kernel_spmd(nc, [arrays], core_ids=[0])
    return r.results[0]["out_0"]
```
